# Optimizing a Trainium2 kernel written in Bass

```python
import numpy as np
import jax
import jax.numpy as jnp

def _softmax(x, axis=-1):
    return jax.nn.softmax(x, axis=axis)

def _gelu(x):
    return jax.nn.gelu(x, approximate=True)

def _silu(x):
    return jax.nn.silu(x)

def _sigmoid(x):
    return jax.nn.sigmoid(x)

def _layernorm(x, axis=-1, eps=1e-05):
    m = jnp.mean(x, axis=axis, keepdims=True)
    v = jnp.var(x, axis=axis, keepdims=True)
    return (x - m) / jnp.sqrt(v + eps)

def _scatter_add(tgt, idx, src, axis=0):
    return tgt.at[idx].add(src)

def _segment_sum(src, seg, n):
    return jax.ops.segment_sum(src, seg, n)
kernel_name = 'mk_sandwich_d1_jaxref_r8_6a6fe5'

def setup_inputs(seed: int=0):
    np.random.seed(seed)
    _w = jnp.asarray

    def _L0_attn_setup():
        import jax, jax.numpy as jnp
        import numpy as np
        import math
        H = 16
        SEG = 128
        DIL = 2

        def hilbert_perm(M: int) -> jnp.ndarray:
            g = int(math.ceil(math.sqrt(M)))
            grid = np.arange(g * g).reshape(g, g)
            grid[1::2] = grid[1::2, ::-1]
            flat = grid.reshape(-1)
            flat = flat[flat < M][:M]
            return jnp.asarray(flat, dtype=jnp.int32)
        key = jax.random.key(seed)
        kx, kq, ko = jax.random.split(key, 3)
        B, M, D = (4, 512, 128)
        x = jax.random.normal(kx, (B, M, D), dtype=jnp.float32)
        w_qkv = jax.random.normal(kq, (3 * D, D), dtype=jnp.float32) * D ** (-0.5)
        w_out = jax.random.normal(ko, (D, D), dtype=jnp.float32) * D ** (-0.5)
        return {'x': x, 'w_qkv': w_qkv, 'w_out': w_out}
    _L0_attn_in = _L0_attn_setup()

    def _L0_ffn_setup():
        import jax, jax.numpy as jnp
        import numpy as np
        D = 128
        F = 128
        E = 8
        K = 2
        B, T = (2, 256)

        def _moe_forward(x, router_w, w1, w2, shared_gate_up, shared_down, shared_gate_w):
            b, t, d = x.shape
            xf = x.reshape(-1, d)
            n = xf.shape[0]
            logits = xf @ router_w
            probs = jax.nn.softmax(logits, axis=-1)
            topw, topi = jax.lax.top_k(probs, K)
            combine = jnp.zeros((n, E), dtype=probs.dtype).at[jnp.arange(n)[:, None], topi].add(topw)
            h = jax.nn.silu(jnp.einsum('nd,edf->nef', xf, w1))
            ye = jnp.einsum('nef,efd->ned', h, w2)
            routed = jnp.einsum('ne,ned->nd', combine, ye)
            gu = xf @ shared_gate_up
            gate, up = (gu[:, :F], gu[:, F:])
            shared = jax.nn.silu(gate) * up @ shared_down
            shared = jax.nn.sigmoid(xf @ shared_gate_w) * shared
            return (routed + shared).reshape(b, t, d)
        key = jax.random.key(seed)
        ks = jax.random.split(key, 7)
        std = 0.02
        x = jax.random.normal(ks[0], (B, T, D), dtype=jnp.float32)
        router_w = jax.random.normal(ks[1], (D, E), dtype=jnp.float32) * std
        w1 = jax.random.normal(ks[2], (E, D, F), dtype=jnp.float32) * std
        w2 = jax.random.normal(ks[3], (E, F, D), dtype=jnp.float32) * std
        shared_gate_up = jax.random.normal(ks[4], (D, 2 * F), dtype=jnp.float32) * std
        shared_down = jax.random.normal(ks[5], (F, D), dtype=jnp.float32) * std
        shared_gate_w = jax.random.normal(ks[6], (D, 1), dtype=jnp.float32) * std
        return {'x': x, 'router_w': router_w, 'w1': w1, 'w2': w2, 'shared_gate_up': shared_gate_up, 'shared_down': shared_down, 'shared_gate_w': shared_gate_w}
    _L0_ffn_in = _L0_ffn_setup()
    _d = {'L0_attn_x': _L0_attn_in['x'], 'L0_attn_w_qkv': _L0_attn_in['w_qkv'], 'L0_attn_w_out': _L0_attn_in['w_out'], 'L0_ffn_router_w': _L0_ffn_in['router_w'], 'L0_ffn_w1': _L0_ffn_in['w1'], 'L0_ffn_w2': _L0_ffn_in['w2'], 'L0_ffn_shared_gate_up': _L0_ffn_in['shared_gate_up'], 'L0_ffn_shared_down': _L0_ffn_in['shared_down'], 'L0_ffn_shared_gate_w': _L0_ffn_in['shared_gate_w']}
    _x0 = _d['L0_attn_x']
    _d['L0_attn_x'] = jax.random.normal(jax.random.fold_in(jax.random.key(seed), 1), (4, 512, 128), dtype=_x0.dtype)
    del _x0
    return _d

def reference(L0_attn_x, L0_attn_w_qkv, L0_attn_w_out, L0_ffn_router_w, L0_ffn_w1, L0_ffn_w2, L0_ffn_shared_gate_up, L0_ffn_shared_down, L0_ffn_shared_gate_w):

    def _L0_attn_ref(x, w_qkv, w_out):
        import jax, jax.numpy as jnp
        import numpy as np
        import math
        H = 16
        SEG = 128
        DIL = 2

        def hilbert_perm(M: int) -> jnp.ndarray:
            g = int(math.ceil(math.sqrt(M)))
            grid = np.arange(g * g).reshape(g, g)
            grid[1::2] = grid[1::2, ::-1]
            flat = grid.reshape(-1)
            flat = flat[flat < M][:M]
            return jnp.asarray(flat, dtype=jnp.int32)
        B, M, Dm = x.shape
        hd = Dm // H
        scale = hd ** (-0.5)
        S = M // SEG
        qkv = x @ w_qkv.T
        qkv = qkv.reshape(B, M, 3, H, hd)
        q = qkv[:, :, 0].transpose(0, 2, 1, 3)
        k = qkv[:, :, 1].transpose(0, 2, 1, 3)
        v = qkv[:, :, 2].transpose(0, 2, 1, 3)
        perm = hilbert_perm(M)
        qh = q[:, :, perm]
        kh = k[:, :, perm]
        vh = v[:, :, perm]
        qh = qh.reshape(B, H, S, SEG, hd)
        kd = kh.reshape(B, H, S, SEG, hd)[:, :, :, ::DIL]
        vd = vh.reshape(B, H, S, SEG, hd)[:, :, :, ::DIL]
        scores = jnp.einsum('bhsqd,bhskd->bhsqk', qh * scale, kd)
        attn = jax.nn.softmax(scores, axis=-1)
        o = jnp.einsum('bhsqk,bhskd->bhsqd', attn, vd)
        o = o.reshape(B, H, M, hd).transpose(0, 2, 1, 3).reshape(B, M, Dm)
        return o @ w_out.T

    def _L0_ffn_ref(x, router_w, w1, w2, shared_gate_up, shared_down, shared_gate_w):
        import jax, jax.numpy as jnp
        import numpy as np
        D = 128
        F = 128
        E = 8
        K = 2
        B, T = (2, 256)

        def _moe_forward(x, router_w, w1, w2, shared_gate_up, shared_down, shared_gate_w):
            b, t, d = x.shape
            xf = x.reshape(-1, d)
            n = xf.shape[0]
            logits = xf @ router_w
            probs = jax.nn.softmax(logits, axis=-1)
            topw, topi = jax.lax.top_k(probs, K)
            combine = jnp.zeros((n, E), dtype=probs.dtype).at[jnp.arange(n)[:, None], topi].add(topw)
            h = jax.nn.silu(jnp.einsum('nd,edf->nef', xf, w1))
            ye = jnp.einsum('nef,efd->ned', h, w2)
            routed = jnp.einsum('ne,ned->nd', combine, ye)
            gu = xf @ shared_gate_up
            gate, up = (gu[:, :F], gu[:, F:])
            shared = jax.nn.silu(gate) * up @ shared_down
            shared = jax.nn.sigmoid(xf @ shared_gate_w) * shared
            return (routed + shared).reshape(b, t, d)
        return _moe_forward(x, router_w, w1, w2, shared_gate_up, shared_down, shared_gate_w)
    x = L0_attn_x
    x = x + _layernorm(_L0_attn_ref(_layernorm(x, axis=-1), L0_attn_w_qkv, L0_attn_w_out), axis=-1)
    x = x + _layernorm(_L0_ffn_ref(_layernorm(x, axis=-1), L0_ffn_router_w, L0_ffn_w1, L0_ffn_w2, L0_ffn_shared_gate_up, L0_ffn_shared_down, L0_ffn_shared_gate_w), axis=-1)
    return x

_drawn_inputs = setup_inputs


def setup_inputs(seed=0):
    import zlib

    import numpy as np

    out = dict(_drawn_inputs(seed))
    spreads = {}
    factors = {}
    for name, (base, spread) in spreads.items():
        noise = np.random.default_rng([zlib.crc32(name.encode()), seed]).standard_normal(out[name].shape)
        drawn = base * np.exp(spread * noise) if base else spread * noise
        out[name] = jnp.asarray(drawn.astype(out[name].dtype))
    for name, factor in factors.items():
        out[name] = (out[name] * factor).astype(out[name].dtype)
    return out
```

```python
from contextlib import ExitStack

import concourse.bass as bass
from concourse import mybir

F32 = mybir.dt.float32
F32R = mybir.dt.float32r
U32 = mybir.dt.uint32
ACT = mybir.ActivationFunctionType
ALU = mybir.AluOpType
AX = mybir.AxisListType

P = 128
B, T, D = 4, 512, 128
NT = T // P
H, HD = 16, 8
G = 4
HG = H // G
KEYS = 64
KB = NT * KEYS
SNAKE = 23
E = 8
RC = E + 2
VW = 2 * (HD + 1)
QSCALE = float(HD) ** -0.5
EPS = 1e-5
MROW = 96

C_ID, C_SEL = 0, P
C_HM = C_SEL + G * 8 * 32
C_ONE = C_HM + HG
C_VM = C_ONE + G * HG
C_VB = C_VM + 2
C_IO = C_VB + VW
C_END = C_IO + E


def snake_parts():
    rows = T // SNAKE
    return rows - rows % 2, rows * SNAKE


def sh_count(m):
    b, k = divmod(m, E + 2)
    return (E + 1) * b + (1 if k <= 1 else k)


def program(nc, x, w_qkv, w_out, router_w, w1, w2, gate_up, down, gate_w, consts, out):
    rows, tail = snake_parts()
    with ExitStack() as ctx:
        def sb(name, shape, dt=F32):
            return ctx.enter_context(nc.sbuf_tensor(name, shape, dt))

        def sem(name):
            return ctx.enter_context(nc.semaphore(name))

        cst = sb("cst", [P, C_END])
        sel = sb("sel", [P, G, 8, 32], F32R)
        X = sb("X", [P, B, NT, D])
        XN = sb("XN", [P, 2, NT, D])
        xTh = sb("xTh", [P, T], F32R)
        xTl = sb("xTl", [P, T], F32R)
        wqkv_n = sb("wqkv_n", [P, 3, D])
        wqkvh = sb("wqkvh", [P, 3, D], F32R)
        wqkvl = sb("wqkvl", [P, 3, D], F32R)
        wout_n = sb("wout_n", [P, D])
        woT = sb("woT", [P, D])
        qch = sb("qch", [P, T], F32R)
        qcl = sb("qcl", [P, T], F32R)
        kch = sb("kch", [P, KB], F32R)
        kcl = sb("kcl", [P, KB], F32R)
        xkh = sb("xkh", [P, NT, P], F32R)
        xkl = sb("xkl", [P, NT, P], F32R)
        Qs = sb("Qs", [P, 2, G, T], F32R)
        Ks = sb("Ks", [P, G, KB], F32R)
        Kb = sb("Kb", [P, 2, G, NT, HG, KEYS], F32R)
        Vb = sb("Vb", [P, 2, NT, 8, VW])
        negm = sb("negm", [P, 2, NT, H])
        Mq = sb("Mq", [P, 2, NT, P], F32R)
        Pr = sb("Pr", [P, 4, 4, P])
        rden = sb("rden", [P, 2, 2, 2 * H])
        O = sb("O", [P, 2, NT, D])
        oT = sb("oT", [P, T])
        TR = sb("TR", [P, B, NT, D])
        X3 = sb("X3", [P, NT, D])
        XH = sb("XH", [P, B, T], F32R)
        XL = sb("XL", [P, B, T], F32R)
        w1n = sb("w1n", [P, E, D])
        w1h = sb("w1h", [P, E, D], F32R)
        w1l = sb("w1l", [P, E, D], F32R)
        w2n = sb("w2n", [P, E, D])
        gun = sb("gun", [P, 2, D])
        guh = sb("guh", [P, 2, D], F32R)
        gul = sb("gul", [P, 2, D], F32R)
        dwn = sb("dwn", [P, D])
        rwn = sb("rwn", [P, RC])
        rwh = sb("rwh", [P, RC], F32R)
        rwl = sb("rwl", [P, RC], F32R)
        hs = sb("hs", [P, 4, T])
        acc = sb("acc", [P, B, NT, D])
        LG = sb("LG", [P, B, NT, RC])
        DL = sb("DL", [P, B, NT, E])
        EX = sb("EX", [P, B, NT, E])
        EZ = sb("EZ", [P, B, NT, 1])
        PB = sb("PB", [P, B, NT, E])
        M8 = sb("M8", [P, B, NT, 8])
        I8 = sb("I8", [P, B, NT, 8], U32)
        EQ = sb("EQ", [P, B, 2, NT, E])
        CW = sb("CW", [P, B, NT, E])
        nmx = sb("nmx", [P, B, 3, NT])
        SG = sb("SG", [P, B, NT])
        mh = sb("mh", [P, B, NT])
        FO = sb("FO", [P, 2, NT, D])
        ST = sb("ST", [P, 4, B, NT, 6])
        MV = sb("MV", [P, 4, B, NT, 2])
        LV = sb("LV", [P, 4, B, NT])
        Y0 = sb("Y0", [P, 4, B, NT])
        NA = sb("NA", [P, 4, B, 3, NT])
        RS = sb("RS", [P, 4, B, NT])
        NM = sb("NM", [P, 4, B, NT])
        nhalf = sb("nhalf", [P, NT])

        ps = [ctx.enter_context(nc.psum_tensor(f"bank{i}", [P, 512], F32)) for i in range(8)]
        S1, S2 = ps[0:2], ps[2:4]
        PA, PBk = ps[4], ps[5]
        PC, PD = ps[6], ps[7]

        names = ("ld_cst ld_wqkv ld_wout ld_w1 ld_w2 ld_gu ld_dwn ld_rw "
                 "selr kones vones mzero nhalf_set wT woT_ps wTh wTl woTr "
                 "w1hs w1ls guhs guls rwhs rwls rwz "
                 "xn xT_ps xh xl qc xk qh ql kc kh kl v_ps vb qs_ps qs ks_ps ks kb_d kb_p "
                 "s1 mx mq mT_ps mev s2 ex pv rd on oT_ps oTs y tr x3n x3T_ps x3h x3l rt lg "
                 "nx dl e8 ez sm rs8 pb m8 i8 eq eqs cw z1 sg "
                 "h sh hp ys ya f1 f2 mh_s step vs pw").split()
        S = {n: sem(n) for n in names}
        ld_x = [sem(f"ld_x{b}") for b in range(B)]
        st, ag, y0, rs, nm = ([sem(f"{n}{k}") for k in range(4)] for n in ("st", "ag", "y0_", "rs_", "nm_"))
        stored = [sem(f"stored{b}") for b in range(B)]
        lv = [sem(f"lv{k}") for k in range(4)]

        ident = cst[:, C_ID:C_ID + P]
        x_v = x.rearrange("b (t p) d -> b p t d", p=P)
        out_v = out.rearrange("b (t p) d -> b p t d", p=P)

        def bank(t, n, w=P):
            return t[:, 0:n * w].rearrange("p (n w) -> p n w", n=n)

        def snake(src, dst):
            s = src[:, 0:rows * SNAKE].rearrange("p (r two c) -> p r two c", two=2, c=SNAKE)
            d = dst[:, 0:rows * SNAKE].rearrange("p (r two c) -> p r two c", two=2, c=SNAKE)
            return [(s[:, :, 0], d[:, :, 0]), (s[:, :, 1, ::-1], d[:, :, 1]), (src[:, tail:T], dst[:, tail:T])]

        block = ctx.enter_context(nc.Block())

        @block.sync
        def _(sp):
            sp.dma_start(cst[:], consts).then_inc(S["ld_cst"], 16)
            sp.dma_start(wqkv_n[:], w_qkv.rearrange("(c p) d -> p c d", p=P)).then_inc(S["ld_wqkv"], 16)
            for b in range(1, B):
                sp.dma_start(X[:, b], x_v[b]).then_inc(ld_x[b], 16)
            sp.dma_start(w1n[:], w1.rearrange("e d f -> d e f")).then_inc(S["ld_w1"], 16)
            sp.dma_start(w2n[:], w2.rearrange("e f d -> f e d")).then_inc(S["ld_w2"], 16)
            for b in range(B):
                sp.wait_ge(S["f2"], NT * (b + 1))
                sp.dma_start(out_v[b], FO[:, b % 2]).then_inc(stored[b], 16)
            for b in range(B):
                sp.wait_ge(stored[b], 16)

        @block.gpsimd
        def _(pool):
            nc.gpsimd.memset(nhalf[:], -0.5).then_inc(S["nhalf_set"], 1)
            nc.gpsimd.memset(rwn[:, E + 1:RC], 0.0).then_inc(S["rwz"], 1)
            nc.gpsimd.memset(Mq[:].bitcast(F32), 0.0).then_inc(S["mzero"], 1)

            def w_low(lo, full, hi, hs_, n, signal):
                pool.wait_ge(hs_, n)
                nc.gpsimd.tensor_tensor(lo, full, hi.bitcast(F32), ALU.subtract).then_inc(signal, 1)

            def k_blocks(b):
                pool.wait_ge(S["ld_cst"], 16)
                pool.wait_ge(S["ks"], 2 * b + 2)
                if b >= 2:
                    pool.wait_ge(S["s2"], 8 * (b - 1))
                shape = [MROW, NT, HG, KEYS]
                for g in (2, 3):
                    rows_ = Ks[0:MROW, g].bitcast(F32).rearrange("p (s k) -> p s k", s=NT)
                    nc.gpsimd.tensor_tensor(
                        Kb[0:MROW, b % 2, g], rows_.unsqueeze(2).to_broadcast(shape),
                        cst[0:MROW, C_HM:C_HM + HG].unsqueeze(1).unsqueeze(3).to_broadcast(shape),
                        ALU.mult).then_inc(S["kb_p"], 1)

            def key_columns(b):
                if b >= 1:
                    pool.wait_ge(S["v_ps"], b)
                for to, src, done in ((xkh, xTh, "xh"), (xkl, xTl, "xl")):
                    pool.wait_ge(S[done], 3 * (b + 1))
                    nc.gpsimd.tensor_copy(
                        to[:].rearrange("p s (two k) -> p s two k", two=2),
                        src[:, 0:T:2].rearrange("p (s k) -> p s k", s=NT).unsqueeze(2)
                        .to_broadcast([P, NT, 2, KEYS])).then_inc(S["xk"], 1)

            key_columns(0)
            k_blocks(0)
            w_low(rwl[:], rwn[:], rwh[:], S["rwhs"], 1, S["rwls"])
            key_columns(1)
            k_blocks(1)
            w_low(gul[:], gun[:], guh[:], S["guhs"], 1, S["guls"])
            w_low(w1l[:], w1n[:], w1h[:], S["w1hs"], 1, S["w1ls"])
            for b in range(2, B):
                key_columns(b)
                k_blocks(b)
            pool.wait_ge(S["nhalf_set"], 1)
            for b in range(B):
                pool.wait_ge(S["vs"], b + 1)
                nc.gpsimd.tensor_tensor(RS[:, 3, b], LV[:, 3, b], nhalf[:], ALU.pow).then_inc(S["pw"], 1)

        @block.tensor
        def _(pe):
            mm, tp = nc.tensor.matmul, nc.tensor.transpose

            def weights_T():
                pe.wait_ge(S["ld_cst"], 16)
                pe.wait_ge(S["ld_wqkv"], 16)
                for c in range(3):
                    i = tp(PA[:, c * P:(c + 1) * P], wqkv_n[:, c], ident)
                i.then_inc(S["wT"], 1)
                pe.wait_ge(S["ld_wout"], 16)
                tp(PBk[:, 0:P], wout_n[:], ident).then_inc(S["woT_ps"], 1)

            def x_T(b):
                pe.wait_ge(S["xn"], NT * (b + 1))
                if b == 0:
                    pe.wait_ge(S["wTh"], 1)
                    pe.wait_ge(S["wTl"], 1)
                else:
                    pe.wait_ge(S["ks"], 2 * b - 1)
                for t in range(NT):
                    i = tp(PA[:, t * P:(t + 1) * P], XN[:, b % 2, t], ident)
                i.then_inc(S["xT_ps"], 1)

            def split3(out_, wh, wl, vh, vl):
                mm(out_, wh, vh, start=True, stop=False)
                mm(out_, wl, vh, start=False, stop=False)
                return mm(out_, wh, vl, start=False, stop=True)

            def qkv(b):
                pe.wait_ge(S["xh"], 3 * (b + 1))
                pe.wait_ge(S["xl"], 3 * (b + 1))
                if b == 0:
                    pe.wait_ge(S["woTr"], 1)
                else:
                    pe.wait_ge(S["vb"], NT * b)
                split3(PBk[:], wqkvh[:, 0], wqkvl[:, 0], xTh[:], xTl[:]).then_inc(S["qc"], 1)
                split3(PA[:, 0:KB], wqkvh[:, 1], wqkvl[:, 1], xTh[:, 0:T:2], xTl[:, 0:T:2]).then_inc(S["kc"], 1)

            def values(b):
                pe.wait_ge(S["ks"], 2 * b + 2)
                pe.wait_ge(S["xk"], 2 * b + 2)
                for s in range(NT):
                    o = PBk[:, s * P:(s + 1) * P]
                    mm(o, xkh[:, s], wqkvh[:, 2], start=True, stop=False)
                    mm(o, xkh[:, s], wqkvl[:, 2], start=False, stop=False)
                    i = mm(o, xkl[:, s], wqkvh[:, 2], start=False, stop=True)
                i.then_inc(S["v_ps"], 1)

            def select(b):
                if b == 0:
                    pe.wait_ge(S["selr"], 1)
                pe.wait_ge(S["kh"], b + 1)
                pe.wait_ge(S["kl"], b + 1)
                pe.wait_ge(S["ql"], b + 1)
                for g in range(G):
                    if g == 1:
                        pe.wait_ge(S["qh"], b + 1)
                        pe.wait_ge(S["ql"], b + 1)
                    if g >= 2:
                        pe.wait_ge(S["qs"], G * b + g - 1)
                    o = (PA, PBk)[g % 2][0:MROW, :]
                    mm(o, sel[:, g, 0:3], qch[:], start=True, stop=False)
                    mm(o, sel[:, g, 2:5], qcl[:], start=False, stop=True).then_inc(S["qs_ps"], 1)
                for half in range(2):
                    pe.wait_ge(S["qs"], G * b + 3 + half)
                    for g in (0, 1):
                        o = (PA, PBk)[half][0:MROW, g * KB:(g + 1) * KB]
                        mm(o, sel[:, 2 * half + g, 4:7], kch[:], start=True, stop=False)
                        i = mm(o, sel[:, 2 * half + g, 5:8], kcl[:], start=False, stop=True)
                    i.then_inc(S["ks_ps"], 1)

            def scores_q(b, s):
                for half in range(2):
                    n = (b * NT + s) * 2 + half
                    if half == 0:
                        pe.wait_ge(S["qs"], G * (b + 1))
                        pe.wait_ge(S["kb_d"], HG * (b + 1))
                    else:
                        pe.wait_ge(S["kb_p"], 2 * (b + 1))
                    if n >= 2:
                        pe.wait_ge(S["mx"], n - 1)
                    for j in range(2):
                        g = 2 * half + j
                        i = mm(S1[n % 2][:, j * 256:(j + 1) * 256], Qs[0:MROW, b % 2, g, s * P:(s + 1) * P],
                               Kb[0:MROW, b % 2, g, s], start=True, stop=True)
                    i.then_inc(S["s1"], 1)

            def max_T(b):
                pe.wait_ge(S["mq"], 2 * (b + 1))
                if b == 1:
                    pe.wait_ge(S["on"], 2)
                if b >= 2:
                    pe.wait_ge(S["lg"], b - 1)
                for s in range(NT):
                    i = tp(PC[:, s * P:(s + 1) * P], Mq[:, b % 2, s].bitcast(F32), ident)
                i.then_inc(S["mT_ps"], 1)

            def scores_k(b, s):
                for half in range(2):
                    n = (b * NT + s) * 2 + half
                    pe.wait_ge(S["mev"], b + 1)
                    if b == 0 and s == 0 and half == 0:
                        pe.wait_ge(S["kones"], 2 * G)
                    if n >= 2:
                        pe.wait_ge(S["ex"], n - 1)
                    for j in range(4):
                        g, pr = 2 * half + j // 2, j % 2
                        i = mm(S2[n % 2][:, j * P:(j + 1) * P],
                               Kb[:, b % 2, g, s, 2 * pr:2 * pr + 2],
                               Qs[:, b % 2, g, s * P:(s + 1) * P], start=True, stop=True)
                    i.then_inc(S["s2"], 1)

            def attend(b, s):
                o = (PD, PC)[s // 2]
                if s == 0 and b >= 1:
                    pe.wait_ge(S["oTs"], b)
                if s == 2 and b >= 1:
                    pe.wait_ge(S["tr"], NT * b)
                if s == 2 and b == 0:
                    pe.wait_ge(S["mev"], 1)
                pe.wait_ge(S["vb"], NT * (b + 1))
                pe.wait_ge(S["vones"], 2)
                for half in range(2):
                    n = (b * NT + s) * 2 + half
                    pe.wait_ge(S["ex"], n + 1)
                    for j in range(4):
                        c = (s % 2) * 8 * VW + (half * 4 + j) * VW
                        i = mm(o[:, c:c + VW], Pr[:, n % 4, j], Vb[:, b % 2, s, half * 4 + j], start=True, stop=True)
                i.then_inc(S["pv"], 1)

            def project(b):
                pe.wait_ge(S["on"], 2 * (b + 1))
                if b >= 1:
                    pe.wait_ge(S["x3h"], b)
                    pe.wait_ge(S["x3l"], b)
                for s in range(NT):
                    i = tp(PD[:, s * P:(s + 1) * P], O[:, b % 2, s], ident)
                i.then_inc(S["oT_ps"], 1)
                pe.wait_ge(S["oTs"], b + 1)
                pe.wait_ge(S["mev"], min(b + 2, B))
                if b == B - 1:
                    pe.wait_ge(S["lg"], B - 1)
                for s in range(NT):
                    i = mm(PC[:, s * P:(s + 1) * P], oT[:, s * P:(s + 1) * P], woT[:], start=True, stop=True)
                i.then_inc(S["y"], 1)

            def moe_in(b):
                pe.wait_ge(S["x3n"], NT * (b + 1))
                if b + 1 < B:
                    pe.wait_ge(S["on"], 2 * (b + 1) + 1)
                for s in range(NT):
                    i = tp(PD[:, s * P:(s + 1) * P], X3[:, s], ident)
                i.then_inc(S["x3T_ps"], 1)

            def router(b):
                pe.wait_ge(S["x3h"], b + 1)
                pe.wait_ge(S["x3l"], b + 1)
                pe.wait_ge(S["rwhs"], 1)
                pe.wait_ge(S["rwls"], 1)
                if b + 1 < B:
                    pe.wait_ge(S["on"], 2 * (b + 2))
                for s in range(NT):
                    xh, xl = XH[:, b, s * P:(s + 1) * P], XL[:, b, s * P:(s + 1) * P]
                    o = PC[:, s * RC:(s + 1) * RC]
                    mm(o, xh, rwh[:], start=True, stop=False)
                    mm(o, xh, rwl[:], start=False, stop=False)
                    i = mm(o, xl, rwh[:], start=False, stop=True)
                i.then_inc(S["rt"], 1)

            weights_T()
            x_T(0)
            qkv(0)
            select(0)
            values(0)
            for s in range(NT):
                scores_q(0, s)
            for i in range(B + 1):
                if i + 1 < B:
                    x_T(i + 1)
                    if i < B:
                        max_T(i)
                    qkv(i + 1)
                elif i < B:
                    max_T(i)
                if i >= 1:
                    project(i - 1)
                if i + 1 < B:
                    select(i + 1)
                    values(i + 1)
                if i < B:
                    for s in range(NT):
                        scores_k(i, s)
                        if i + 1 < B:
                            scores_q(i + 1, s)
                        if s >= 1:
                            attend(i, s - 1)
                    attend(i, NT - 1)
                if i >= 1:
                    moe_in(i - 1)
                    router(i - 1)

            def hidden(n, wh, wl, b):
                pe_bank = ps[n % 4]
                if n >= 4:
                    m = n - 4
                    pe.wait_ge(S["sh"], sh_count(m))
                    if m % (E + 2) == 1:
                        pe.wait_ge(S["hp"], m // (E + 2) + 1)
                split3(pe_bank[:], wh, wl, XH[:, b], XL[:, b]).then_inc(S["h"], 1)

            def outputs(n, lhs, w):
                pe_bank = ps[4 + n % 4]
                if n >= 4:
                    pe.wait_ge(S["ya"], NT * (n - 3))
                for s in range(NT):
                    i = mm(pe_bank[:, s * P:(s + 1) * P], lhs[:, s * P:(s + 1) * P], w, start=True, stop=True)
                i.then_inc(S["ys"], 1)

            pe.wait_ge(S["mx"], 8 * B)
            pe.wait_ge(S["ex"], 8 * B)
            pe.wait_ge(S["ks"], 2 * B)
            pe.wait_ge(S["lg"], B)
            for n_, k in (("w1hs", 1), ("w1ls", 1), ("guhs", 1), ("guls", 1)):
                pe.wait_ge(S[n_], k)
            pe.wait_ge(S["ld_w2"], 16)
            pe.wait_ge(S["ld_dwn"], 16)
            for b in range(B):
                n0, m0 = (E + 2) * b, (E + 1) * b
                hidden(n0, guh[:, 0], gul[:, 0], b)
                hidden(n0 + 1, guh[:, 1], gul[:, 1], b)
                hidden(n0 + 2, w1h[:, 0], w1l[:, 0], b)
                for e in range(-1, E):
                    if 0 <= e + 1 < E and e >= 0:
                        hidden(n0 + 3 + e, w1h[:, e + 1], w1l[:, e + 1], b)
                    if e < 0:
                        pe.wait_ge(S["hp"], b + 1)
                        outputs(m0, hs[:, 3], dwn[:])
                    else:
                        pe.wait_ge(S["sh"], (E + 1) * b + e + 2)
                        outputs(m0 + 1 + e, hs[:, e % 3], w2n[:, e])

        @block.scalar
        def _(act):
            A = nc.scalar.activation
            act.dma_start(X[:, 0], x_v[0]).then_inc(ld_x[0], 16)
            act.dma_start(wout_n[:], w_out).then_inc(S["ld_wout"], 16)
            act.dma_start(gun[:], gate_up.rearrange("d (c f) -> d c f", c=2)).then_inc(S["ld_gu"], 16)
            act.dma_start(dwn[:], down).then_inc(S["ld_dwn"], 16)
            act.dma_start(rwn[:, 0:E], router_w).then_inc(S["ld_rw"], 16)
            act.dma_start(rwn[:, E:E + 1], gate_w).then_inc(S["ld_rw"], 16)

            def ln_seed(k, b):
                act.wait_ge(ag[k], NT * (b + 1))
                A(LV[:, k, b], NA[:, k, b, 0], ACT.Ln).then_inc(lv[k], 1)
                act.wait_ge(lv[k], b + 1)
                A(Y0[:, k, b], LV[:, k, b], ACT.Exp, scale=-0.5).then_inc(y0[k], 1)

            def normalise_x(b):
                act.wait_ge(nm[0], b + 1)
                act.wait_ge(ld_x[b], 16)
                if b >= 2:
                    act.wait_ge(S["xT_ps"], b - 1)
                for t in range(NT):
                    A(XN[:, b % 2, t], X[:, b, t], ACT.Identity, scale=RS[:, 0, b, t:t + 1],
                      bias=NM[:, 0, b, t:t + 1]).then_inc(S["xn"], 1)

            def x_high(b):
                act.wait_ge(S["xT_ps"], b + 1)
                if b >= 1:
                    act.wait_ge(S["kc"], b)
                    act.wait_ge(S["xk"], 2 * b)
                for s_, d_ in snake(PA, xTh):
                    A(d_, s_, ACT.Copy).then_inc(S["xh"], 1)

            def max_rows(b):
                act.wait_ge(S["mT_ps"], b + 1)
                src = PC[MROW:P, 0:T].unsqueeze(1).to_broadcast([P - MROW, G, T])
                if b >= 2:
                    act.wait_ge(S["s2"], 8 * (b - 1))
                A(Qs[MROW:P, b % 2], src, ACT.Copy).then_inc(S["mev"], 1)

            def qk_high(b):
                act.wait_ge(S["qc"], b + 1)
                if b >= 1:
                    act.wait_ge(S["qs_ps"], G * b)
                A(qch[:], PBk[:], ACT.Copy, scale=QSCALE).then_inc(S["qh"], 1)
                act.wait_ge(S["kc"], b + 1)
                if b >= 1:
                    act.wait_ge(S["ks_ps"], 2 * b)
                A(kch[:], PA[:, 0:KB], ACT.Copy).then_inc(S["kh"], 1)

            def o_copy(b):
                act.wait_ge(S["oT_ps"], b + 1)
                if b >= 1:
                    act.wait_ge(S["y"], b)
                A(oT[:], PD[:], ACT.Copy).then_inc(S["oTs"], 1)

            def qk_rows(b):
                if b >= 2:
                    act.wait_ge(S["s2"], 8 * (b - 1))
                for g in range(G):
                    act.wait_ge(S["qs_ps"], G * b + g + 1)
                    A(Qs[0:MROW, b % 2, g], (PA, PBk)[g % 2][0:MROW, :], ACT.Copy).then_inc(S["qs"], 1)
                for half in range(2):
                    act.wait_ge(S["ks_ps"], 2 * b + half + 1)
                    if b >= 1:
                        act.wait_ge(*((S["kb_d"], HG * b) if half == 0 else (S["kb_p"], 2 * b)))
                    A(Ks[0:MROW, 2 * half:2 * half + 2], (PA, PBk)[half][0:MROW, :].rearrange(
                        "p (g n) -> p g n", g=2), ACT.Copy).then_inc(S["ks"], 1)

            def exps(b, s):
                for half in range(2):
                    n = (b * NT + s) * 2 + half
                    act.wait_ge(S["s2"], n + 1)
                    if n >= 4:
                        act.wait_ge(S["pv"], (n - 4) // 2 + 1)
                    A(Pr[:, n % 4], bank(S2[n % 2], 4), ACT.Exp).then_inc(S["ex"], 1)

            def normalise_3(b):
                act.wait_ge(nm[2], b + 1)
                if b >= 1:
                    act.wait_ge(S["x3T_ps"], b)
                for t in range(NT):
                    A(X3[:, t], TR[:, b, t], ACT.Identity, scale=RS[:, 2, b, t:t + 1],
                      bias=NM[:, 2, b, t:t + 1]).then_inc(S["x3n"], 1)

            def x3_high(b):
                act.wait_ge(S["x3T_ps"], b + 1)
                A(XH[:, b], PD[:], ACT.Copy).then_inc(S["x3h"], 1)

            def router_exp(b):
                act.wait_ge(S["dl"], b + 1)
                A(EX[:, b], DL[:, b], ACT.Exp).then_inc(S["e8"], 1)
                A(EZ[:, b], LG[:, b, :, E:E + 1], ACT.Exp, scale=-1.0).then_inc(S["ez"], 1)

            act.wait_ge(S["wT"], 1)
            A(wqkvh[:], bank(PA, 3), ACT.Copy).then_inc(S["wTh"], 1)
            act.wait_ge(S["woT_ps"], 1)
            A(woT[:], PBk[:, 0:P], ACT.Copy).then_inc(S["woTr"], 1)
            act.wait_ge(S["ld_cst"], 16)
            for u in range(2):
                for g in range(G):
                    A(Kb[MROW:P, u, g], cst[MROW:P, C_ONE + g * HG:C_ONE + (g + 1) * HG].unsqueeze(1).unsqueeze(3)
                      .to_broadcast([P - MROW, NT, HG, KEYS]), ACT.Copy).then_inc(S["kones"], 1)
            ln_seed(0, 0)
            normalise_x(0)
            x_high(0)
            qk_high(0)
            qk_rows(0)
            act.wait_ge(S["ld_rw"], 32)
            act.wait_ge(S["rwz"], 1)
            A(rwh[:], rwn[:], ACT.Copy).then_inc(S["rwhs"], 1)
            act.wait_ge(S["ld_gu"], 16)
            A(guh[:], gun[:], ACT.Copy).then_inc(S["guhs"], 1)
            act.wait_ge(S["ld_w1"], 16)
            A(w1h[:], w1n[:], ACT.Copy).then_inc(S["w1hs"], 1)
            ln_seed(0, 1)
            normalise_x(1)
            for i in range(B + 1):
                if i + 1 < B:
                    x_high(i + 1)
                if i < B:
                    max_rows(i)
                if i + 1 < B:
                    qk_high(i + 1)
                if i >= 1:
                    o_copy(i - 1)
                if i + 1 < B:
                    qk_rows(i + 1)
                if i >= 1:
                    ln_seed(1, i - 1)
                if i < B:
                    exps(i, 0)
                    exps(i, 1)
                if i >= 1:
                    ln_seed(2, i - 1)
                    normalise_3(i - 1)
                if i < B:
                    exps(i, 2)
                    exps(i, 3)
                if i + 2 < B:
                    ln_seed(0, i + 2)
                    normalise_x(i + 2)
                if i >= 1:
                    x3_high(i - 1)
                    router_exp(i - 1)

            for b in range(B):
                for k in range(-1, E):
                    n = (E + 2) * b + (0 if k < 0 else k + 2)
                    act.wait_ge(S["h"], n + 1)
                    if k < 0:
                        if b >= 1:
                            act.wait_ge(S["ys"], (E + 1) * (b - 1) + 1)
                        A(hs[:, 3], ps[n % 4][:], ACT.Silu).then_inc(S["sh"], 1)
                    else:
                        if k >= 3:
                            act.wait_ge(S["ys"], (E + 1) * b + k - 1)
                        elif b >= 1:
                            last = max(e for e in range(E) if e % 3 == k)
                            act.wait_ge(S["ys"], (E + 1) * (b - 1) + last + 2)
                        A(hs[:, k % 3], ps[n % 4][:], ACT.Silu).then_inc(S["sh"], 1)

        @block.vector
        def _(dve):
            V = nc.vector
            steps = [0]

            def link(ins):
                steps[0] += 1
                ins.then_inc(S["step"], 1)
                dve.wait_ge(S["step"], steps[0])

            def stats(k, b, tiles):
                for t in range(NT):
                    V.bn_stats(ST[:, k, b, t], tiles[t]).then_inc(st[k], 1)
                for t in range(NT):
                    dve.wait_ge(st[k], NT * b + t + 1)
                    i = V.bn_aggr(MV[:, k, b, t], ST[:, k, b, t])
                    if t < NT - 1:
                        i.then_inc(ag[k], 1)
                    else:
                        link(i)
                V.tensor_scalar(NA[:, k, b, 0], MV[:, k, b, :, 1], EPS, None, ALU.add).then_inc(ag[k], 1)

            def refine(k, b):
                dve.wait_ge(y0[k], b + 1)
                link(V.tensor_tensor(NA[:, k, b, 1], NA[:, k, b, 0], Y0[:, k, b], ALU.mult))
                link(V.tensor_tensor(NA[:, k, b, 2], NA[:, k, b, 1], Y0[:, k, b], ALU.mult))
                link(V.tensor_scalar(NA[:, k, b, 1], NA[:, k, b, 2], -0.5, 1.5, ALU.mult, ALU.add))
                V.tensor_tensor(RS[:, k, b], NA[:, k, b, 1], Y0[:, k, b], ALU.mult).then_inc(rs[k], 1)
                dve.wait_ge(rs[k], b + 1)
                V.scalar_tensor_tensor(out=NM[:, k, b], in0=MV[:, k, b, :, 0], scalar=-1.0, in1=RS[:, k, b],
                                       op0=ALU.mult, op1=ALU.mult).then_inc(nm[k], 1)

            def stats_x(b):
                dve.wait_ge(ld_x[b], 16)
                stats(0, b, [X[:, b, t] for t in range(NT)])
                refine(0, b)

            def x_low(b):
                dve.wait_ge(S["xh"], 3 * (b + 1))
                if b >= 1:
                    dve.wait_ge(S["kc"], b)
                    dve.wait_ge(S["xk"], 2 * b)
                for (s_, d_), (_, h_) in zip(snake(PA, xTl), snake(PA, xTh)):
                    V.tensor_tensor(d_, s_, h_.bitcast(F32), ALU.subtract).then_inc(S["xl"], 1)

            def qk_low(b):
                dve.wait_ge(S["qh"], b + 1)
                V.scalar_tensor_tensor(out=qcl[:], in0=PBk[:], scalar=QSCALE, in1=qch[:].bitcast(F32),
                                       op0=ALU.mult, op1=ALU.subtract).then_inc(S["ql"], 1)
                dve.wait_ge(S["kh"], b + 1)
                V.tensor_tensor(kcl[:], PA[:, 0:KB], kch[:].bitcast(F32), ALU.subtract).then_inc(S["kl"], 1)

            def v_blocks(b):
                dve.wait_ge(S["v_ps"], b + 1)
                if b >= 2:
                    dve.wait_ge(S["pv"], NT * (b - 1))
                m = cst[:, C_VM:C_VM + 2].unsqueeze(1).unsqueeze(3).to_broadcast([P, 8, 2, HD])
                for s in range(NT):
                    o = Vb[:, b % 2, s].rearrange("p j (two c) -> p j two c", two=2)[:, :, :, 0:HD]
                    v = PBk[:, s * P:(s + 1) * P].rearrange("p (j two c) -> p j two c", two=2, c=HD)
                    V.tensor_tensor(o, v, m, ALU.mult).then_inc(S["vb"], 1)

            def k_blocks(b):
                dve.wait_ge(S["ks"], 2 * b + 1)
                if b >= 2:
                    dve.wait_ge(S["s2"], 8 * (b - 1))
                for h in range(HG):
                    V.tensor_scalar(Kb[0:MROW, b % 2, 0:2, :, h].rearrange("p g s k -> p (g s) k"),
                                    Ks[0:MROW, 0:2].bitcast(F32).rearrange("p g (s k) -> p (g s) k", k=KEYS),
                                    cst[0:MROW, C_HM + h:C_HM + h + 1], None, ALU.mult).then_inc(S["kb_d"], 1)

            def maxima(b, s):
                for half in range(2):
                    n = (b * NT + s) * 2 + half
                    dve.wait_ge(S["s1"], n + 1)
                    V.tensor_reduce(negm[:, b % 2, s, 8 * half:8 * half + 8], bank(S1[n % 2], 8, KEYS), AX.X,
                                    ALU.max, negate=True).then_inc(S["mx"], 1)

            def max_split(b):
                dve.wait_ge(S["mx"], 8 * (b + 1))
                if b == 0:
                    dve.wait_ge(S["mzero"], 1)
                V.tensor_copy(Mq[:, b % 2, :, MROW:MROW + H], negm[:, b % 2]).then_inc(S["mq"], 1)
                dve.wait_ge(S["mq"], 2 * b + 1)
                V.tensor_tensor(Mq[:, b % 2, :, MROW + H:P], negm[:, b % 2],
                                Mq[:, b % 2, :, MROW:MROW + H].bitcast(F32), ALU.subtract).then_inc(S["mq"], 1)

            def divide(b, c):
                dve.wait_ge(S["pv"], NT * b + 2 * c + 2)
                o = (PD, PC)[c][:, 0:2 * 8 * VW].rearrange("p (n w) -> p n w", w=HD + 1)
                V.reciprocal(rden[:, b % 2, c], o[:, :, HD]).then_inc(S["rd"], 1)
                dve.wait_ge(S["rd"], 2 * b + c + 1)
                V.tensor_tensor(O[:, b % 2, 2 * c:2 * c + 2].rearrange("p s (h d) -> p (s h) d", d=HD), o[:, :, 0:HD],
                                rden[:, b % 2, c].unsqueeze(2).to_broadcast([P, 2 * H, HD]),
                                ALU.mult).then_inc(S["on"], 1)

            def residual(b):
                dve.wait_ge(S["y"], b + 1)
                stats(1, b, [PC[:, t * P:(t + 1) * P] for t in range(NT)])

            def residual2(b):
                refine(1, b)
                for t in range(NT):
                    V.scalar_tensor_tensor(out=TR[:, b, t], in0=PC[:, t * P:(t + 1) * P], scalar=RS[:, 1, b, t:t + 1],
                                           in1=X[:, b, t], op0=ALU.mult, op1=ALU.add).then_inc(S["tr"], 1)
                dve.wait_ge(S["tr"], NT * (b + 1))
                stats(2, b, [TR[:, b, t] for t in range(NT)])

            def x3_low(b):
                dve.wait_ge(S["x3h"], b + 1)
                V.tensor_tensor(XL[:, b], PD[:], XH[:, b].bitcast(F32), ALU.subtract).then_inc(S["x3l"], 1)

            def route(b):
                dve.wait_ge(S["rt"], b + 1)
                V.tensor_copy(LG[:, b], bank(PC, NT, RC)).then_inc(S["lg"], 1)
                dve.wait_ge(S["lg"], b + 1)
                V.tensor_reduce(nmx[:, b, 0], LG[:, b, :, 0:E], AX.X, ALU.max, negate=True).then_inc(S["nx"], 1)
                dve.wait_ge(S["nx"], b + 1)
                V.tensor_tensor(DL[:, b], LG[:, b, :, 0:E], nmx[:, b, 0].unsqueeze(2).to_broadcast([P, NT, E]),
                                ALU.add).then_inc(S["dl"], 1)

            def route2(b):
                def wide(a):
                    return a.unsqueeze(2).to_broadcast([P, NT, E])

                dve.wait_ge(S["ez"], b + 1)
                V.tensor_reduce(nmx[:, b, 1], EX[:, b], AX.X, ALU.add).then_inc(S["sm"], 1)
                link(V.tensor_scalar(EZ[:, b], EZ[:, b], 1.0, None, ALU.add))
                V.reciprocal(SG[:, b], EZ[:, b, :, 0]).then_inc(S["sg"], 1)
                link(V.reciprocal(nmx[:, b, 2], nmx[:, b, 1]))
                V.tensor_tensor(PB[:, b], EX[:, b], wide(nmx[:, b, 2]), ALU.mult).then_inc(S["pb"], 1)
                dve.wait_ge(S["pb"], b + 1)
                for t in range(NT):
                    V.max(M8[:, b, t], PB[:, b, t]).then_inc(S["m8"], 1)
                for t in range(NT):
                    dve.wait_ge(S["m8"], NT * b + t + 1)
                    V.max_index(I8[:, b, t], M8[:, b, t], PB[:, b, t]).then_inc(S["i8"], 1)
                dve.wait_ge(S["i8"], NT * (b + 1))
                iota = cst[:, C_IO:C_IO + E].unsqueeze(1).to_broadcast([P, NT, E])
                for j in range(2):
                    V.tensor_tensor(EQ[:, b, j], iota, wide(I8[:, b, :, j]), ALU.is_equal).then_inc(S["eq"], 1)
                dve.wait_ge(S["eq"], 2 * (b + 1))
                link(V.tensor_tensor(EQ[:, b, 0], EQ[:, b, 0], EQ[:, b, 1], ALU.add))
                V.tensor_tensor(CW[:, b], EQ[:, b, 0], PB[:, b], ALU.mult).then_inc(S["cw"], 1)

            dve.wait_ge(S["ld_cst"], 16)
            stats_x(0)
            dve.wait_ge(S["wTh"], 1)
            V.tensor_tensor(wqkvl[:], bank(PA, 3), wqkvh[:].bitcast(F32), ALU.subtract).then_inc(S["wTl"], 1)
            V.tensor_copy(sel[:].rearrange("p g b c -> p (g b c)"), cst[:, C_SEL:C_HM]).then_inc(S["selr"], 1)
            for u in range(2):
                V.tensor_copy(Vb[:, u].rearrange("p s j c -> p (s j) c"),
                              cst[:, C_VB:C_VB + VW].unsqueeze(1).to_broadcast([P, NT * 8, VW])).then_inc(S["vones"], 1)
            dve.wait_ge(S["vones"], 2)
            x_low(0)
            qk_low(0)
            stats_x(1)
            k_blocks(0)
            v_blocks(0)
            for s in range(NT):
                maxima(0, s)
            max_split(0)
            for i in range(B + 1):
                if i + 1 < B:
                    x_low(i + 1)
                    qk_low(i + 1)
                if i >= 1:
                    residual(i - 1)
                if i + 1 < B:
                    k_blocks(i + 1)
                    v_blocks(i + 1)
                    maxima(i + 1, 0)
                if i >= 1:
                    residual2(i - 1)
                if i + 1 < B:
                    maxima(i + 1, 1)
                if i >= 1:
                    refine(2, i - 1)
                if i < B:
                    divide(i, 0)
                if i + 1 < B:
                    maxima(i + 1, 2)
                    maxima(i + 1, 3)
                    max_split(i + 1)
                if i + 2 < B:
                    stats_x(i + 2)
                if i < B:
                    divide(i, 1)
                if i >= 1:
                    x3_low(i - 1)
                    route(i - 1)
                    route2(i - 1)

            def accumulate(b, k):
                n = (E + 1) * b + k + 1
                dve.wait_ge(S["ys"], n + 1)
                if k < 0:
                    dve.wait_ge(S["sg"], b + 1)
                if k == 0:
                    dve.wait_ge(S["cw"], b + 1)
                for t in range(NT):
                    y = ps[4 + n % 4][:, t * P:(t + 1) * P]
                    if k < 0:
                        V.tensor_scalar(acc[:, b, t], y, SG[:, b, t:t + 1], None, ALU.mult).then_inc(S["ya"], 1)
                    else:
                        dve.wait_ge(S["ya"], NT * (n - 1) + t + 1)
                        V.scalar_tensor_tensor(out=acc[:, b, t], in0=y, scalar=CW[:, b, t, k:k + 1],
                                               in1=acc[:, b, t], op0=ALU.mult, op1=ALU.add).then_inc(S["ya"], 1)

            def norm_out(b):
                dve.wait_ge(S["ya"], NT * (E + 1) * (b + 1))
                for t in range(NT):
                    V.bn_stats(ST[:, 3, b, t], acc[:, b, t]).then_inc(st[3], 1)
                for t in range(NT):
                    dve.wait_ge(st[3], NT * b + t + 1)
                    V.bn_aggr(MV[:, 3, b, t], ST[:, 3, b, t]).then_inc(ag[3], 1)
                dve.wait_ge(ag[3], NT * (b + 1))
                V.tensor_scalar(LV[:, 3, b], MV[:, 3, b, :, 1], EPS, None, ALU.add).then_inc(S["vs"], 1)

            def finish(b):
                dve.wait_ge(S["pw"], b + 1)
                V.tensor_tensor(mh[:, b], MV[:, 3, b, :, 0], RS[:, 3, b], ALU.mult).then_inc(S["mh_s"], 1)
                if b >= 2:
                    dve.wait_ge(stored[b - 2], 16)
                for t in range(NT):
                    V.scalar_tensor_tensor(out=acc[:, b, t], in0=acc[:, b, t], scalar=RS[:, 3, b, t:t + 1],
                                           in1=TR[:, b, t], op0=ALU.mult, op1=ALU.add).then_inc(S["f1"], 1)
                dve.wait_ge(S["mh_s"], b + 1)
                link(V.tensor_tensor(mh[:, b], NM[:, 1, b], mh[:, b], ALU.subtract))
                for t in range(NT):
                    dve.wait_ge(S["f1"], NT * b + t + 1)
                    V.tensor_scalar(FO[:, b % 2, t], acc[:, b, t], mh[:, b, t:t + 1], None,
                                    ALU.add).then_inc(S["f2"], 1)

            for b in range(B):
                n = (E + 2) * b + 1
                dve.wait_ge(S["h"], n + 1)
                dve.wait_ge(S["sh"], (E + 1) * b + 1)
                V.tensor_tensor(hs[:, 3], ps[n % 4][:], hs[:, 3], ALU.mult).then_inc(S["hp"], 1)
                accumulate(b, -1)
                accumulate(b, 0)
                if b >= 1:
                    finish(b - 1)
                for k in range(1, E):
                    accumulate(b, k)
                norm_out(b)
            finish(B - 1)


def constants():
    import numpy as np
    c = np.zeros((P, C_END), np.float32)
    eye = np.eye(P, dtype=np.float32)
    c[:, C_ID:C_ID + P] = eye
    for g in range(G):
        for j in (0, 1, 4, 6):
            at = C_SEL + (g * 8 + j) * 32
            c[:, at:at + 32] = eye[:, 32 * g:32 * g + 32]
    p = np.arange(P)
    for h in range(HG):
        c[:MROW, C_HM + h] = (p[:MROW] % 32) // HD == h
    for h in range(H):
        c[MROW:, C_ONE + h] = (p[MROW:] - MROW) % H == h
    for j in range(2):
        half = (p // KEYS == j).astype(np.float32)
        c[:, C_VM + j] = half
        c[:, C_VB + j * (HD + 1) + HD] = half
    c[:, C_IO:C_IO + E] = np.arange(E)
    return c


_INS = ["L0_attn_x", "L0_attn_w_qkv", "L0_attn_w_out", "L0_ffn_router_w", "L0_ffn_w1", "L0_ffn_w2",
        "L0_ffn_shared_gate_up", "L0_ffn_shared_down", "L0_ffn_shared_gate_w"]


def kernel(**inputs):
    import numpy as np
    import concourse.bacc as bacc
    from concourse.bass_utils import run_bass_kernel_spmd as run

    nc = bacc.Bacc("TRN2", target_bir_lowering=False, num_devices=1)
    arrays, args = {}, []
    named = [(n, np.ascontiguousarray(inputs[n])) for n in _INS] + [("consts", constants())]
    for n, a in named:
        arrays[f"in_{n}"] = a
        args.append(nc.dram_tensor(f"in_{n}", a.shape, mybir.dt.from_np(a.dtype), kind="ExternalInput").ap())
    out = nc.dram_tensor("out", (B, T, D), F32, kind="ExternalOutput").ap()
    program(nc, *args, out)
    r = run(nc, [arrays], core_ids=[0])
    return r.results[0]["out"]
```

```python
from contextlib import ExitStack

import concourse.bass as bass
from concourse import mybir

F32 = mybir.dt.float32
F32R = mybir.dt.float32r
U32 = mybir.dt.uint32
ACT = mybir.ActivationFunctionType
ALU = mybir.AluOpType
AX = mybir.AxisListType

P = 128
B, T, D = 4, 512, 128
NT = T // P
H, HD = 16, 8
G = 4
HG = H // G
KEYS = 64
KB = NT * KEYS
SNAKE = 23
E = 8
RC = E + 2
VW = 32
QSCALE = float(HD) ** -0.5
EPS = 1e-5
MROW = 96

C_ID, C_SEL = 0, P
C_HM = C_SEL + G * 8 * 32
C_ONE = C_HM + HG
C_VM = C_ONE + G * HG
C_VB = C_VM + 2
C_IO = C_VB + VW
C_END = C_IO + E


def snake_parts():
    rows = T // SNAKE
    return rows - rows % 2, rows * SNAKE


def sh_count(m):
    b, k = divmod(m, E + 2)
    return (E + 1) * b + (1 if k <= 1 else k)


def program(nc, x, w_qkv, w_out, router_w, w1, w2, gate_up, down, gate_w, consts, out):
    rows, tail = snake_parts()
    with ExitStack() as ctx:
        def sb(name, shape, dt=F32):
            return ctx.enter_context(nc.sbuf_tensor(name, shape, dt))

        def sem(name):
            return ctx.enter_context(nc.semaphore(name))

        cst = sb("cst", [P, C_END])
        sel = sb("sel", [P, G, 8, 32], F32R)
        X = sb("X", [P, B, NT, D])
        XN = sb("XN", [P, 2, NT, D])
        xTh = sb("xTh", [P, T], F32R)
        xTl = sb("xTl", [P, T], F32R)
        wqkv_n = sb("wqkv_n", [P, 3, D])
        wqkvh = sb("wqkvh", [P, 3, D], F32R)
        wqkvl = sb("wqkvl", [P, 3, D], F32R)
        wout_n = sb("wout_n", [P, D])
        woT = sb("woT", [P, D])
        qch = sb("qch", [P, T], F32R)
        qcl = sb("qcl", [P, T], F32R)
        kch = sb("kch", [P, KB], F32R)
        kcl = sb("kcl", [P, KB], F32R)
        xkh = sb("xkh", [P, NT, P], F32R)
        xkl = sb("xkl", [P, NT, P], F32R)
        Qs = sb("Qs", [P, 2, G, T], F32R)
        Ks = sb("Ks", [P, G, KB], F32R)
        Kb = sb("Kb", [P, 2, G, NT, HG, KEYS], F32R)
        Vb = sb("Vb", [P, 2, NT, H // 2, VW])
        AVs = sb("AVs", [P, 2, 2 * P])
        kone = sb("kone", [P, G, HG, KEYS], F32R)
        negm = sb("negm", [P, 2, NT, H])
        Mq = sb("Mq", [P, 2, NT, P], F32R)
        Pr = sb("Pr", [P, 4, 4, P])
        rden = sb("rden", [P, 2, 2, H, 2])
        O = sb("O", [P, 2, NT, D])
        oT = sb("oT", [P, T])
        TR = sb("TR", [P, B, NT, D])
        X3 = sb("X3", [P, NT, D])
        XH = sb("XH", [P, B, T], F32R)
        XL = sb("XL", [P, B, T], F32R)
        w1n = sb("w1n", [P, E, D])
        w1h = sb("w1h", [P, E, D], F32R)
        w1l = sb("w1l", [P, E, D], F32R)
        w2n = sb("w2n", [P, E, D])
        gun = sb("gun", [P, 2, D])
        guh = sb("guh", [P, 2, D], F32R)
        gul = sb("gul", [P, 2, D], F32R)
        dwn = sb("dwn", [P, D])
        rwn = sb("rwn", [P, RC])
        rwh = sb("rwh", [P, RC], F32R)
        rwl = sb("rwl", [P, RC], F32R)
        hs = Pr[:].rearrange("p n j q -> p n (j q)")
        acc = X
        FO = XN
        LG = sb("LG", [P, B, NT, RC])
        DL = sb("DL", [P, B, NT, E])
        EX = sb("EX", [P, B, NT, E])
        EZ = sb("EZ", [P, B, NT, 1])
        PB = sb("PB", [P, B, NT, E])
        M8 = sb("M8", [P, B, NT, 8])
        I8 = sb("I8", [P, B, NT, 8], U32)
        EQ = sb("EQ", [P, B, 2, NT, E])
        CW = sb("CW", [P, B, NT, E])
        nmx = sb("nmx", [P, B, 3, NT])
        SG = sb("SG", [P, B, NT])
        mh = sb("mh", [P, B, NT])
        ST = sb("ST", [P, 4, B, NT, 6])
        MV = sb("MV", [P, 4, B, NT, 2])
        VE = sb("VE", [P, 4, B, NT])
        RS = sb("RS", [P, 4, B, NT])
        NM = sb("NM", [P, 4, B, NT])
        nhalf = sb("nhalf", [P, NT])

        ps = [ctx.enter_context(nc.psum_tensor(f"bank{i}", [P, 512], F32)) for i in range(8)]
        S1, S2 = ps[0:2], ps[2:4]
        PA, PBk = ps[4], ps[5]
        PC, PD = ps[6], ps[7]

        names = ("ld_cst ld_wqkv ld_wout ld_w1 ld_w2 ld_gu ld_dwn ld_rw "
                 "selr kones vones mzero nhalf_set wT woT_ps wTh wTl woTr "
                 "w1hs w1ls guhs guls rwhs rwls rwz "
                 "xn xT_ps xh xl qc xk qh ql kc kh kl v_ps vb qs_ps qs ks_ps ks kb_d kb_p "
                 "s1 mx mq mT_ps mev s2 ex pv avc at rd on oT_ps oTs y tr x3n x3T_ps x3h x3l rt lg "
                 "nx dl e8 ez sm rs8 pb m8 i8 eq eqs cw z1 sg "
                 "h sh hp ys ya f1 f2 mh_s step").split()
        S = {n: sem(n) for n in names}
        ld_x = [sem(f"ld_x{b}") for b in range(B)]
        st, ag, ve, pw, nm = ([sem(f"{n}{k}") for k in range(4)] for n in ("st", "ag", "ve", "pw", "nm"))
        stored = [sem(f"stored{b}") for b in range(B)]
        ld_id, kdma = sem("ld_id"), sem("kdma")

        ident = cst[:, C_ID:C_ID + P]
        x_v = x.rearrange("b (t p) d -> b p t d", p=P)
        out_v = out.rearrange("b (t p) d -> b p t d", p=P)

        def bank(t, n, w=P):
            return t[:, 0:n * w].rearrange("p (n w) -> p n w", n=n)

        def snake(src, dst):
            s = src[:, 0:rows * SNAKE].rearrange("p (r two c) -> p r two c", two=2, c=SNAKE)
            d = dst[:, 0:rows * SNAKE].rearrange("p (r two c) -> p r two c", two=2, c=SNAKE)
            return [(s[:, :, 0], d[:, :, 0]), (s[:, :, 1, ::-1], d[:, :, 1]), (src[:, tail:T], dst[:, tail:T])]

        block = ctx.enter_context(nc.Block())

        @block.sync
        def _(sp):
            sp.dma_start(wqkv_n[:], w_qkv.rearrange("(c p) d -> p c d", p=P)).then_inc(S["ld_wqkv"], 16)
            sp.dma_start(cst[:, P:C_END], consts[:, P:C_END]).then_inc(S["ld_cst"], 16)
            for b in range(1, B):
                sp.dma_start(X[:, b], x_v[b]).then_inc(ld_x[b], 16)
            sp.dma_start(w1n[:], w1.rearrange("e d f -> d e f")).then_inc(S["ld_w1"], 16)
            sp.dma_start(w2n[:], w2.rearrange("e f d -> f e d")).then_inc(S["ld_w2"], 16)
            sp.wait_ge(S["kones"], 1)
            for u in range(2):
                for s in range(NT):
                    sp.dma_start(Kb[MROW:P, u, :, s].bitcast(F32), kone[MROW:P].bitcast(F32)).then_inc(kdma, 16)
            for b in range(B):
                sp.wait_ge(S["f2"], NT * (b + 1))
                sp.dma_start(out_v[b], FO[:, b % 2]).then_inc(stored[b], 16)
            for b in range(B):
                sp.wait_ge(stored[b], 16)

        @block.gpsimd
        def _(pool):
            nc.gpsimd.memset(nhalf[:], -0.5).then_inc(S["nhalf_set"], 1)
            nc.gpsimd.memset(rwn[:, E + 1:RC], 0.0).then_inc(S["rwz"], 1)
            nc.gpsimd.memset(Mq[:].bitcast(F32), 0.0).then_inc(S["mzero"], 1)

            def w_low(lo, full, hi, hs_, n, signal):
                pool.wait_ge(hs_, n)
                nc.gpsimd.tensor_tensor(lo, full, hi.bitcast(F32), ALU.subtract).then_inc(signal, 1)

            def k_blocks(b):
                pool.wait_ge(S["ld_cst"], 16)
                pool.wait_ge(S["ks"], 2 * b + 2)
                if b >= 2:
                    pool.wait_ge(S["s2"], 8 * (b - 1))
                shape = [MROW, NT, HG, KEYS]
                for g in (2, 3):
                    rows_ = Ks[0:MROW, g].bitcast(F32).rearrange("p (s k) -> p s k", s=NT)
                    nc.gpsimd.tensor_tensor(
                        Kb[0:MROW, b % 2, g], rows_.unsqueeze(2).to_broadcast(shape),
                        cst[0:MROW, C_HM:C_HM + HG].unsqueeze(1).unsqueeze(3).to_broadcast(shape),
                        ALU.mult).then_inc(S["kb_p"], 1)

            def key_columns(b):
                if b >= 1:
                    pool.wait_ge(S["v_ps"], b)
                for to, src, done in ((xkh, xTh, "xh"), (xkl, xTl, "xl")):
                    pool.wait_ge(S[done], 3 * (b + 1))
                    nc.gpsimd.tensor_copy(
                        to[:].rearrange("p s (two k) -> p s two k", two=2),
                        src[:, 0:T:2].rearrange("p (s k) -> p s k", s=NT).unsqueeze(2)
                        .to_broadcast([P, NT, 2, KEYS])).then_inc(S["xk"], 1)

            def powers(k, b, n=1):
                pool.wait_ge(ve[k], b + n)
                if k == 0 and b == 0:
                    pool.wait_ge(S["nhalf_set"], 1)
                for c in range(b, b + n):
                    nc.gpsimd.tensor_tensor(RS[:, k, c], VE[:, k, c], nhalf[:], ALU.pow).then_inc(pw[k], 1)

            powers(0, 0)
            powers(0, 1)
            key_columns(0)
            k_blocks(0)
            powers(0, 2)
            powers(0, 3)
            key_columns(1)
            for i in range(B + 1):
                if i + 1 < B:
                    k_blocks(i + 1)
                if i == 0:
                    w_low(rwl[:], rwn[:], rwh[:], S["rwhs"], 1, S["rwls"])
                    w_low(gul[:], gun[:], guh[:], S["guhs"], 1, S["guls"])
                if i >= 1:
                    powers(1, i - 1)
                    powers(2, i - 1)
                if i + 2 < B:
                    key_columns(i + 2)
                if i == 0:
                    w_low(w1l[:], w1n[:], w1h[:], S["w1hs"], 1, S["w1ls"])
            for b in range(B):
                powers(3, b)

        @block.tensor
        def _(pe):
            mm, tp = nc.tensor.matmul, nc.tensor.transpose

            def weights_T():
                pe.wait_ge(ld_id, 16)
                pe.wait_ge(S["ld_wqkv"], 16)
                for c in range(3):
                    i = tp(PA[:, c * P:(c + 1) * P], wqkv_n[:, c], ident)
                i.then_inc(S["wT"], 1)
                pe.wait_ge(S["ld_wout"], 16)
                tp(PBk[:, 0:P], wout_n[:], ident).then_inc(S["woT_ps"], 1)

            def x_T(b):
                pe.wait_ge(S["xn"], NT * (b + 1))
                if b == 0:
                    pe.wait_ge(S["wTh"], 1)
                    pe.wait_ge(S["wTl"], 1)
                else:
                    pe.wait_ge(S["qs"], G * b - 1)
                for t in range(NT):
                    i = tp(PA[:, t * P:(t + 1) * P], XN[:, b % 2, t], ident)
                i.then_inc(S["xT_ps"], 1)

            def split3(out_, wh, wl, vh, vl):
                mm(out_, wh, vh, start=True, stop=False)
                mm(out_, wl, vh, start=False, stop=False)
                return mm(out_, wh, vl, start=False, stop=True)

            def qkv(b):
                pe.wait_ge(S["xh"], 3 * (b + 1))
                pe.wait_ge(S["xl"], 3 * (b + 1))
                if b == 0:
                    pe.wait_ge(S["woTr"], 1)
                else:
                    pe.wait_ge(S["vb"], NT * b)
                split3(PBk[:], wqkvh[:, 0], wqkvl[:, 0], xTh[:], xTl[:]).then_inc(S["qc"], 1)
                split3(PA[:, 0:KB], wqkvh[:, 1], wqkvl[:, 1], xTh[:, 0:T:2], xTl[:, 0:T:2]).then_inc(S["kc"], 1)

            def select_k(b):
                if b == 0:
                    pe.wait_ge(S["selr"], 1)
                pe.wait_ge(S["kh"], b + 1)
                pe.wait_ge(S["kl"], b + 1)
                for half in range(2):
                    if half == 1:
                        pe.wait_ge(S["qh"], b + 1)
                        pe.wait_ge(S["ql"], b + 1)
                    for g in (0, 1):
                        o = (PA, PBk)[half][0:MROW, g * KB:(g + 1) * KB]
                        mm(o, sel[:, 2 * half + g, 4:7], kch[:], start=True, stop=False)
                        i = mm(o, sel[:, 2 * half + g, 5:8], kcl[:], start=False, stop=True)
                    i.then_inc(S["ks_ps"], 1)

            def select_q(b, g):
                if g < 2:
                    pe.wait_ge(S["ks"], 2 * b + g + 1)
                else:
                    pe.wait_ge(S["qs"], G * b + g - 1)
                o = (PA, PBk)[g % 2][0:MROW, :]
                mm(o, sel[:, g, 0:3], qch[:], start=True, stop=False)
                mm(o, sel[:, g, 2:5], qcl[:], start=False, stop=True).then_inc(S["qs_ps"], 1)

            def values(b):
                pe.wait_ge(S["qs"], G * b + G)
                pe.wait_ge(S["xk"], 2 * b + 2)
                for s in range(NT):
                    o = PBk[:, s * P:(s + 1) * P]
                    mm(o, xkh[:, s], wqkvh[:, 2], start=True, stop=False)
                    mm(o, xkh[:, s], wqkvl[:, 2], start=False, stop=False)
                    i = mm(o, xkl[:, s], wqkvh[:, 2], start=False, stop=True)
                i.then_inc(S["v_ps"], 1)

            def scores_q(b, s):
                for half in range(2):
                    n = (b * NT + s) * 2 + half
                    if half == 0:
                        pe.wait_ge(S["qs"], G * (b + 1))
                        pe.wait_ge(S["kb_d"], HG * (b + 1))
                    else:
                        pe.wait_ge(S["kb_p"], 2 * (b + 1))
                    if n >= 2:
                        pe.wait_ge(S["mx"], n - 1)
                    if s == 0 and b >= 2:
                        if half == 0:
                            pe.wait_ge(S["tr"], NT * (b - 1))
                        elif b >= 3:
                            pe.wait_ge(S["lg"], b - 2)
                    for j in range(2):
                        g = 2 * half + j
                        i = mm(S1[n % 2][:, j * 256:(j + 1) * 256], Qs[0:MROW, b % 2, g, s * P:(s + 1) * P],
                               Kb[0:MROW, b % 2, g, s], start=True, stop=True)
                    i.then_inc(S["s1"], 1)

            def max_T(b):
                pe.wait_ge(S["mq"], 2 * (b + 1))
                if b >= 1:
                    pe.wait_ge(S["avc"], NT * b)
                for s in range(NT):
                    i = tp(PC[:, s * P:(s + 1) * P], Mq[:, b % 2, s].bitcast(F32), ident)
                i.then_inc(S["mT_ps"], 1)

            def scores_k(b, s):
                for half in range(2):
                    n = (b * NT + s) * 2 + half
                    pe.wait_ge(S["mev"], 2 * b + half + 1)
                    if b == 0 and s == 0 and half == 0:
                        pe.wait_ge(kdma, 16 * 2 * NT)
                    if n >= 2:
                        pe.wait_ge(S["ex"], n - 1)
                    for j in range(4):
                        g, pr = 2 * half + j // 2, j % 2
                        i = mm(S2[n % 2][:, j * P:(j + 1) * P],
                               Kb[:, b % 2, g, s, 2 * pr:2 * pr + 2],
                               Qs[:, b % 2, g, s * P:(s + 1) * P], start=True, stop=True)
                    i.then_inc(S["s2"], 1)

            def attend(b, s):
                if s == 0:
                    pe.wait_ge(S["mev"], 2 * b + 2)
                if NT * b + s >= 1:
                    pe.wait_ge(S["avc"], NT * b + s)
                pe.wait_ge(S["vb"], NT * (b + 1))
                pe.wait_ge(S["vones"], 2)
                for half in range(2):
                    n = (b * NT + s) * 2 + half
                    pe.wait_ge(S["ex"], n + 1)
                    for j in range(4):
                        i = mm(PC[j * VW:(j + 1) * VW, (s % 2) * 2 * P + half * P:(s % 2) * 2 * P + (half + 1) * P],
                               Vb[:, b % 2, s, half * 4 + j], Pr[:, n % 4, j], start=True, stop=True)
                i.then_inc(S["pv"], 1)

            def attend_T(b, s):
                pe.wait_ge(S["avc"], NT * b + s + 1)
                if s == 0 and b >= 1:
                    pe.wait_ge(S["oTs"], b)
                if s == 2:
                    pe.wait_ge(S["on"], 2 * b + 1)
                for half in range(2):
                    c = (s % 2) * 2 * P + half * P
                    i = tp(PD[:, c:c + P], AVs[:, s % 2, half * P:(half + 1) * P], ident)
                i.then_inc(S["at"], 1)

            def output_T(b):
                pe.wait_ge(S["on"], 2 * (b + 1))
                for s in range(NT):
                    i = tp(PD[:, s * P:(s + 1) * P], O[:, b % 2, s], ident)
                i.then_inc(S["oT_ps"], 1)

            def project(b):
                pe.wait_ge(S["oTs"], b + 1)
                pe.wait_ge(S["mx"], 8 * min(b + 2, B))
                for s in range(NT):
                    i = mm(S1[0][:, s * P:(s + 1) * P], oT[:, s * P:(s + 1) * P], woT[:], start=True, stop=True)
                i.then_inc(S["y"], 1)

            def moe_in(b):
                pe.wait_ge(S["x3n"], NT * (b + 1))
                pe.wait_ge(S["mx"], 8 * min(b + 3, B))
                for s in range(NT):
                    i = tp(S1[1][:, s * P:(s + 1) * P], X3[:, s], ident)
                i.then_inc(S["x3T_ps"], 1)

            def router(b):
                pe.wait_ge(S["x3h"], b + 1)
                pe.wait_ge(S["x3l"], b + 1)
                pe.wait_ge(S["rwhs"], 1)
                pe.wait_ge(S["rwls"], 1)
                for s in range(NT):
                    xh, xl = XH[:, b, s * P:(s + 1) * P], XL[:, b, s * P:(s + 1) * P]
                    o = S1[1][:, s * RC:(s + 1) * RC]
                    mm(o, xh, rwh[:], start=True, stop=False)
                    mm(o, xh, rwl[:], start=False, stop=False)
                    i = mm(o, xl, rwh[:], start=False, stop=True)
                i.then_inc(S["rt"], 1)

            weights_T()
            x_T(0)
            qkv(0)
            select_k(0)
            for g in range(G):
                select_q(0, g)
            values(0)
            x_T(1)
            scores_q(0, 0)
            qkv(1)
            for s in range(1, NT):
                scores_q(0, s)
            for i in range(B):
                p1, p2 = i + 2 < B, i + 1 < B
                if i >= 2:
                    moe_in(i - 2)
                max_T(i)
                if p2:
                    select_k(i + 1)
                if i >= 1:
                    output_T(i - 1)
                if p2:
                    select_q(i + 1, 0)
                    select_q(i + 1, 1)
                scores_k(i, 0)
                if i >= 2:
                    router(i - 2)
                if i >= 1:
                    project(i - 1)
                if p2:
                    select_q(i + 1, 2)
                    select_q(i + 1, 3)
                scores_k(i, 1)
                attend(i, 0)
                if p2:
                    values(i + 1)
                if p1:
                    x_T(i + 2)
                scores_k(i, 2)
                attend_T(i, 0)
                attend(i, 1)
                if p2:
                    scores_q(i + 1, 0)
                if p1:
                    qkv(i + 2)
                scores_k(i, 3)
                attend_T(i, 1)
                attend(i, 2)
                if p2:
                    scores_q(i + 1, 1)
                    scores_q(i + 1, 2)
                attend_T(i, 2)
                attend(i, 3)
                if p2:
                    scores_q(i + 1, 3)
                attend_T(i, 3)

            def hidden(n, wh, wl, b):
                if n >= 3:
                    m = n - 3
                    pe.wait_ge(S["sh"], sh_count(m))
                    if m % (E + 2) == 1:
                        pe.wait_ge(S["hp"], m // (E + 2) + 1)
                split3(ps[2 + n % 3][:], wh, wl, XH[:, b], XL[:, b]).then_inc(S["h"], 1)

            def outputs(n, lhs, w):
                if n >= 3:
                    pe.wait_ge(S["ya"], NT * (n - 2))
                for s in range(NT):
                    i = mm(ps[5 + n % 3][:, s * P:(s + 1) * P], lhs[:, s * P:(s + 1) * P], w, start=True, stop=True)
                i.then_inc(S["ys"], 1)

            moe_in(B - 2)
            output_T(B - 1)
            pe.wait_ge(S["ex"], 8 * B)
            pe.wait_ge(S["qs"], G * B)
            pe.wait_ge(S["vb"], NT * B)
            pe.wait_ge(S["avc"], NT * B)
            for n_ in ("w1hs", "w1ls", "guhs", "guls"):
                pe.wait_ge(S[n_], 1)
            pe.wait_ge(S["ld_w2"], 16)
            pe.wait_ge(S["ld_dwn"], 16)
            for b in range(B):
                n0, m0 = (E + 2) * b, (E + 1) * b
                hidden(n0, guh[:, 0], gul[:, 0], b)
                hidden(n0 + 1, guh[:, 1], gul[:, 1], b)
                if b == 0:
                    router(B - 2)
                    project(B - 1)
                hidden(n0 + 2, w1h[:, 0], w1l[:, 0], b)
                pe.wait_ge(S["hp"], b + 1)
                outputs(m0, hs[:, 3], dwn[:])
                for e in range(E):
                    if e + 1 < E:
                        hidden(n0 + 3 + e, w1h[:, e + 1], w1l[:, e + 1], b)
                    pe.wait_ge(S["sh"], (E + 1) * b + e + 2)
                    outputs(m0 + 1 + e, hs[:, e % 3], w2n[:, e])
                    if b == 0 and e == 4:
                        moe_in(B - 1)
                    if b == 0 and e == 6:
                        router(B - 1)

        @block.scalar
        def _(act):
            A = nc.scalar.activation
            act.dma_start(X[:, 0], x_v[0]).then_inc(ld_x[0], 16)
            act.dma_start(cst[:, 0:P], consts[:, 0:P]).then_inc(ld_id, 16)
            act.dma_start(wout_n[:], w_out).then_inc(S["ld_wout"], 16)
            act.dma_start(gun[:], gate_up.rearrange("d (c f) -> d c f", c=2)).then_inc(S["ld_gu"], 16)
            act.dma_start(dwn[:], down).then_inc(S["ld_dwn"], 16)
            act.dma_start(rwn[:, 0:E], router_w).then_inc(S["ld_rw"], 16)
            act.dma_start(rwn[:, E:E + 1], gate_w).then_inc(S["ld_rw"], 16)

            def normalise_x(b):
                act.wait_ge(nm[0], b + 1)
                act.wait_ge(ld_x[b], 16)
                if b >= 2:
                    act.wait_ge(S["xT_ps"], b - 1)
                for t in range(NT):
                    A(XN[:, b % 2, t], X[:, b, t], ACT.Identity, scale=RS[:, 0, b, t:t + 1],
                      bias=NM[:, 0, b, t:t + 1]).then_inc(S["xn"], 1)

            def x_high(b):
                act.wait_ge(S["xT_ps"], b + 1)
                if b >= 1:
                    act.wait_ge(S["kc"], b)
                    act.wait_ge(S["xk"], 2 * b)
                for s_, d_ in snake(PA, xTh):
                    A(d_, s_, ACT.Copy).then_inc(S["xh"], 1)

            def max_rows(b, half):
                act.wait_ge(S["mT_ps"], b + 1)
                src = PC[MROW:P, 0:T].unsqueeze(1).to_broadcast([P - MROW, 2, T])
                if b >= 2:
                    act.wait_ge(S["s2"], 8 * (b - 1))
                A(Qs[MROW:P, b % 2, 2 * half:2 * half + 2], src, ACT.Copy).then_inc(S["mev"], 1)

            def qk_high(b):
                act.wait_ge(S["qc"], b + 1)
                if b >= 1:
                    act.wait_ge(S["qs_ps"], G * b)
                A(qch[:], PBk[:], ACT.Copy, scale=QSCALE).then_inc(S["qh"], 1)
                act.wait_ge(S["kc"], b + 1)
                if b >= 1:
                    act.wait_ge(S["ks_ps"], 2 * b)
                A(kch[:], PA[:, 0:KB], ACT.Copy).then_inc(S["kh"], 1)

            def o_copy(b):
                act.wait_ge(S["oT_ps"], b + 1)
                if b >= 1:
                    act.wait_ge(S["y"], b)
                A(oT[:], PD[:], ACT.Copy).then_inc(S["oTs"], 1)

            def q_rows(b, g):
                if b >= 2:
                    act.wait_ge(S["s2"], 8 * (b - 1))
                act.wait_ge(S["qs_ps"], G * b + g + 1)
                A(Qs[0:MROW, b % 2, g], (PA, PBk)[g % 2][0:MROW, :], ACT.Copy).then_inc(S["qs"], 1)

            def k_rows(b, half):
                act.wait_ge(S["ks_ps"], 2 * b + half + 1)
                if b >= 1:
                    act.wait_ge(*((S["kb_d"], HG * b) if half == 0 else (S["kb_p"], 2 * b)))
                A(Ks[0:MROW, 2 * half:2 * half + 2], (PA, PBk)[half][0:MROW, :].rearrange(
                    "p (g n) -> p g n", g=2), ACT.Copy).then_inc(S["ks"], 1)

            def attended(b, s):
                n = NT * b + s
                act.wait_ge(S["pv"], n + 1)
                if n >= 2:
                    act.wait_ge(S["at"], n - 1)
                A(AVs[:, s % 2], PC[:, (s % 2) * 2 * P:(s % 2 + 1) * 2 * P], ACT.Copy).then_inc(S["avc"], 1)

            def exps(b, s):
                for half in range(2):
                    n = (b * NT + s) * 2 + half
                    act.wait_ge(S["s2"], n + 1)
                    if n >= 4:
                        act.wait_ge(S["pv"], (n - 4) // 2 + 1)
                    A(Pr[:, n % 4], bank(S2[n % 2], 4), ACT.Exp).then_inc(S["ex"], 1)

            def normalise_3(b):
                act.wait_ge(nm[2], b + 1)
                if b >= 1:
                    act.wait_ge(S["x3T_ps"], b)
                for t in range(NT):
                    A(X3[:, t], TR[:, b, t], ACT.Identity, scale=RS[:, 2, b, t:t + 1],
                      bias=NM[:, 2, b, t:t + 1]).then_inc(S["x3n"], 1)

            def x3_high(b):
                act.wait_ge(S["x3T_ps"], b + 1)
                A(XH[:, b], S1[1][:], ACT.Copy).then_inc(S["x3h"], 1)

            def router_exp(b):
                act.wait_ge(S["dl"], b + 1)
                A(EX[:, b], DL[:, b], ACT.Exp).then_inc(S["e8"], 1)
                A(EZ[:, b], LG[:, b, :, E:E + 1], ACT.Exp, scale=-1.0).then_inc(S["ez"], 1)

            act.wait_ge(S["wT"], 1)
            A(wqkvh[:], bank(PA, 3), ACT.Copy).then_inc(S["wTh"], 1)
            act.wait_ge(S["woT_ps"], 1)
            A(woT[:], PBk[:, 0:P], ACT.Copy).then_inc(S["woTr"], 1)
            normalise_x(0)
            x_high(0)
            act.wait_ge(S["ld_cst"], 16)
            A(kone[MROW:P], cst[MROW:P, C_ONE:C_ONE + G * HG].rearrange("p (g h) -> p g h", g=G).unsqueeze(3)
              .to_broadcast([P - MROW, G, HG, KEYS]), ACT.Copy).then_inc(S["kones"], 1)
            qk_high(0)
            k_rows(0, 0)
            k_rows(0, 1)
            for g in range(G):
                q_rows(0, g)
            normalise_x(1)
            x_high(1)
            act.wait_ge(S["ld_rw"], 32)
            act.wait_ge(S["rwz"], 1)
            A(rwh[:], rwn[:], ACT.Copy).then_inc(S["rwhs"], 1)
            act.wait_ge(S["ld_gu"], 16)
            A(guh[:], gun[:], ACT.Copy).then_inc(S["guhs"], 1)
            qk_high(1)
            act.wait_ge(S["ld_w1"], 16)
            A(w1h[:], w1n[:], ACT.Copy).then_inc(S["w1hs"], 1)
            normalise_x(2)
            for i in range(B):
                p1, p2 = i + 2 < B, i + 1 < B
                if i >= 2:
                    x3_high(i - 2)
                if p2:
                    k_rows(i + 1, 0)
                max_rows(i, 0)
                if p2:
                    k_rows(i + 1, 1)
                max_rows(i, 1)
                if i >= 1:
                    o_copy(i - 1)
                if p2:
                    q_rows(i + 1, 0)
                    q_rows(i + 1, 1)
                exps(i, 0)
                if p2:
                    q_rows(i + 1, 2)
                    q_rows(i + 1, 3)
                if i >= 2:
                    router_exp(i - 2)
                exps(i, 1)
                attended(i, 0)
                exps(i, 2)
                if p1:
                    x_high(i + 2)
                attended(i, 1)
                if i >= 1:
                    normalise_3(i - 1)
                exps(i, 3)
                if p1:
                    qk_high(i + 2)
                attended(i, 2)
                attended(i, 3)
                if i + 3 < B:
                    normalise_x(i + 3)

            x3_high(B - 2)
            o_copy(B - 1)
            router_exp(B - 2)

            for b in range(B):
                for k in range(-1, E):
                    n = (E + 2) * b + (0 if k < 0 else k + 2)
                    act.wait_ge(S["h"], n + 1)
                    if k < 0:
                        if b >= 1:
                            act.wait_ge(S["ys"], (E + 1) * (b - 1) + 1)
                        A(hs[:, 3], ps[2 + n % 3][:], ACT.Silu).then_inc(S["sh"], 1)
                    else:
                        if k >= 3:
                            act.wait_ge(S["ys"], (E + 1) * b + k - 1)
                        elif b >= 1:
                            last = max(e for e in range(E) if e % 3 == k)
                            act.wait_ge(S["ys"], (E + 1) * (b - 1) + last + 2)
                        A(hs[:, k % 3], ps[2 + n % 3][:], ACT.Silu).then_inc(S["sh"], 1)
                    if b == 0 and k == 3:
                        normalise_3(B - 1)
                    if b == 0 and k == 6:
                        x3_high(B - 1)
                if b == 0:
                    router_exp(B - 1)

        @block.vector
        def _(dve):
            V = nc.vector
            steps = [0]

            def link(ins):
                steps[0] += 1
                ins.then_inc(S["step"], 1)
                dve.wait_ge(S["step"], steps[0])

            def stats(k, b, tiles):
                for t in range(NT):
                    V.bn_stats(ST[:, k, b, t], tiles[t]).then_inc(st[k], 1)
                for t in range(NT):
                    dve.wait_ge(st[k], NT * b + t + 1)
                    V.bn_aggr(MV[:, k, b, t], ST[:, k, b, t]).then_inc(ag[k], 1)
                dve.wait_ge(ag[k], NT * (b + 1))
                V.tensor_scalar(VE[:, k, b], MV[:, k, b, :, 1], EPS, None, ALU.add).then_inc(ve[k], 1)

            def neg_mean(k, b):
                dve.wait_ge(pw[k], b + 1)
                V.scalar_tensor_tensor(out=NM[:, k, b], in0=MV[:, k, b, :, 0], scalar=-1.0, in1=RS[:, k, b],
                                       op0=ALU.mult, op1=ALU.mult).then_inc(nm[k], 1)

            def stats_x(b):
                dve.wait_ge(ld_x[b], 16)
                stats(0, b, [X[:, b, t] for t in range(NT)])

            def x_low(b):
                dve.wait_ge(S["xh"], 3 * (b + 1))
                if b >= 1:
                    dve.wait_ge(S["kc"], b)
                    dve.wait_ge(S["xk"], 2 * b)
                for (s_, d_), (_, h_) in zip(snake(PA, xTl), snake(PA, xTh)):
                    V.tensor_tensor(d_, s_, h_.bitcast(F32), ALU.subtract).then_inc(S["xl"], 1)

            def qk_low(b):
                dve.wait_ge(S["qh"], b + 1)
                V.scalar_tensor_tensor(out=qcl[:], in0=PBk[:], scalar=QSCALE, in1=qch[:].bitcast(F32),
                                       op0=ALU.mult, op1=ALU.subtract).then_inc(S["ql"], 1)
                dve.wait_ge(S["kh"], b + 1)
                V.tensor_tensor(kcl[:], PA[:, 0:KB], kch[:].bitcast(F32), ALU.subtract).then_inc(S["kl"], 1)

            def v_blocks(b):
                dve.wait_ge(S["v_ps"], b + 1)
                if b >= 2:
                    dve.wait_ge(S["pv"], NT * (b - 1))
                m = cst[:, C_VM:C_VM + 2].unsqueeze(1).unsqueeze(3).to_broadcast([P, 8, 2, HD])
                for s in range(NT):
                    o = Vb[:, b % 2, s, :, 0:2 * HD].rearrange("p j (two c) -> p j two c", two=2)
                    v = PBk[:, s * P:(s + 1) * P].rearrange("p (j two c) -> p j two c", two=2, c=HD)
                    V.tensor_tensor(o, v, m, ALU.mult).then_inc(S["vb"], 1)

            def k_blocks(b):
                dve.wait_ge(S["ks"], 2 * b + 1)
                if b >= 2:
                    dve.wait_ge(S["s2"], 8 * (b - 1))
                for h in range(HG):
                    V.tensor_scalar(Kb[0:MROW, b % 2, 0:2, :, h].rearrange("p g s k -> p (g s) k"),
                                    Ks[0:MROW, 0:2].bitcast(F32).rearrange("p g (s k) -> p (g s) k", k=KEYS),
                                    cst[0:MROW, C_HM + h:C_HM + h + 1], None, ALU.mult).then_inc(S["kb_d"], 1)

            def maxima(b, s):
                for half in range(2):
                    n = (b * NT + s) * 2 + half
                    dve.wait_ge(S["s1"], n + 1)
                    V.tensor_reduce(negm[:, b % 2, s, 8 * half:8 * half + 8], bank(S1[n % 2], 8, KEYS), AX.X,
                                    ALU.max, negate=True).then_inc(S["mx"], 1)

            def max_split(b):
                dve.wait_ge(S["mx"], 8 * (b + 1))
                if b == 0:
                    dve.wait_ge(S["mzero"], 1)
                V.tensor_copy(Mq[:, b % 2, :, MROW:MROW + H], negm[:, b % 2]).then_inc(S["mq"], 1)
                dve.wait_ge(S["mq"], 2 * b + 1)
                V.tensor_tensor(Mq[:, b % 2, :, MROW + H:P], negm[:, b % 2],
                                Mq[:, b % 2, :, MROW:MROW + H].bitcast(F32), ALU.subtract).then_inc(S["mq"], 1)

            def divide(b, c):
                dve.wait_ge(S["at"], NT * b + 2 * c + 2)
                o = PD[:].rearrange("p (j w) -> p j w", w=VW)
                V.reciprocal(rden[:, b % 2, c], o[:, :, 2 * HD:2 * HD + 2]).then_inc(S["rd"], 1)
                dve.wait_ge(S["rd"], 2 * b + c + 1)
                V.tensor_tensor(O[:, b % 2, 2 * c:2 * c + 2].rearrange("p s (j two d) -> p (s j) two d", two=2, d=HD),
                                o[:, :, 0:2 * HD].rearrange("p j (two d) -> p j two d", two=2),
                                rden[:, b % 2, c].unsqueeze(3).to_broadcast([P, H, 2, HD]),
                                ALU.mult).then_inc(S["on"], 1)

            def residual(b):
                dve.wait_ge(S["y"], b + 1)
                stats(1, b, [S1[0][:, t * P:(t + 1) * P] for t in range(NT)])

            def residual2(b):
                neg_mean(1, b)
                for t in range(NT):
                    V.scalar_tensor_tensor(out=TR[:, b, t], in0=S1[0][:, t * P:(t + 1) * P], scalar=RS[:, 1, b, t:t + 1],
                                           in1=X[:, b, t], op0=ALU.mult, op1=ALU.add).then_inc(S["tr"], 1)
                dve.wait_ge(S["tr"], NT * (b + 1))
                stats(2, b, [TR[:, b, t] for t in range(NT)])

            def x3_low(b):
                dve.wait_ge(S["x3h"], b + 1)
                V.tensor_tensor(XL[:, b], S1[1][:], XH[:, b].bitcast(F32), ALU.subtract).then_inc(S["x3l"], 1)

            def route(b):
                dve.wait_ge(S["rt"], b + 1)
                V.tensor_copy(LG[:, b], bank(S1[1], NT, RC)).then_inc(S["lg"], 1)
                dve.wait_ge(S["lg"], b + 1)
                V.tensor_reduce(nmx[:, b, 0], LG[:, b, :, 0:E], AX.X, ALU.max, negate=True).then_inc(S["nx"], 1)
                dve.wait_ge(S["nx"], b + 1)
                V.tensor_tensor(DL[:, b], LG[:, b, :, 0:E], nmx[:, b, 0].unsqueeze(2).to_broadcast([P, NT, E]),
                                ALU.add).then_inc(S["dl"], 1)

            def route2(b):
                def wide(a):
                    return a.unsqueeze(2).to_broadcast([P, NT, E])

                dve.wait_ge(S["ez"], b + 1)
                V.tensor_reduce(nmx[:, b, 1], EX[:, b], AX.X, ALU.add).then_inc(S["sm"], 1)
                link(V.tensor_scalar(EZ[:, b], EZ[:, b], 1.0, None, ALU.add))
                V.reciprocal(SG[:, b], EZ[:, b, :, 0]).then_inc(S["sg"], 1)
                link(V.reciprocal(nmx[:, b, 2], nmx[:, b, 1]))
                V.tensor_tensor(PB[:, b], EX[:, b], wide(nmx[:, b, 2]), ALU.mult).then_inc(S["pb"], 1)
                dve.wait_ge(S["pb"], b + 1)
                for t in range(NT):
                    V.max(M8[:, b, t], PB[:, b, t]).then_inc(S["m8"], 1)
                for t in range(NT):
                    dve.wait_ge(S["m8"], NT * b + t + 1)
                    V.max_index(I8[:, b, t], M8[:, b, t], PB[:, b, t]).then_inc(S["i8"], 1)
                dve.wait_ge(S["i8"], NT * (b + 1))
                iota = cst[:, C_IO:C_IO + E].unsqueeze(1).to_broadcast([P, NT, E])
                for j in range(2):
                    V.tensor_tensor(EQ[:, b, j], iota, wide(I8[:, b, :, j]), ALU.is_equal).then_inc(S["eq"], 1)
                dve.wait_ge(S["eq"], 2 * (b + 1))
                link(V.tensor_tensor(EQ[:, b, 0], EQ[:, b, 0], EQ[:, b, 1], ALU.add))
                V.tensor_tensor(CW[:, b], EQ[:, b, 0], PB[:, b], ALU.mult).then_inc(S["cw"], 1)

            stats_x(0)
            stats_x(1)
            dve.wait_ge(S["wTh"], 1)
            V.tensor_tensor(wqkvl[:], bank(PA, 3), wqkvh[:].bitcast(F32), ALU.subtract).then_inc(S["wTl"], 1)
            neg_mean(0, 0)
            neg_mean(0, 1)
            dve.wait_ge(S["ld_cst"], 16)
            V.tensor_copy(sel[:].rearrange("p g b c -> p (g b c)"), cst[:, C_SEL:C_HM]).then_inc(S["selr"], 1)
            x_low(0)
            qk_low(0)
            for u in range(2):
                V.tensor_copy(Vb[:, u].rearrange("p s j c -> p (s j) c"), cst[:, C_VB:C_VB + VW].unsqueeze(1)
                              .to_broadcast([P, NT * H // 2, VW])).then_inc(S["vones"], 1)
            k_blocks(0)
            stats_x(2)
            dve.wait_ge(S["vones"], 2)
            v_blocks(0)
            stats_x(3)
            maxima(0, 0)
            neg_mean(0, 2)
            x_low(1)
            maxima(0, 1)
            qk_low(1)
            maxima(0, 2)
            maxima(0, 3)
            max_split(0)
            neg_mean(0, 3)
            for i in range(B):
                p1, p2 = i + 2 < B, i + 1 < B
                if i >= 2:
                    x3_low(i - 2)
                if p2:
                    k_blocks(i + 1)
                if i >= 2:
                    route(i - 2)
                if i >= 1:
                    residual(i - 1)
                if p2:
                    v_blocks(i + 1)
                if i >= 1:
                    residual2(i - 1)
                if i >= 2:
                    route2(i - 2)
                if p2:
                    maxima(i + 1, 0)
                if i >= 1:
                    neg_mean(2, i - 1)
                if p1:
                    x_low(i + 2)
                if p2:
                    maxima(i + 1, 1)
                divide(i, 0)
                if p1:
                    qk_low(i + 2)
                if p2:
                    maxima(i + 1, 2)
                    maxima(i + 1, 3)
                    max_split(i + 1)
                divide(i, 1)

            x3_low(B - 2)
            route(B - 2)

            def accumulate(b, k):
                n = (E + 1) * b + k + 1
                dve.wait_ge(S["ys"], n + 1)
                if k < 0:
                    dve.wait_ge(S["sg"], b + 1)
                if k == 0:
                    dve.wait_ge(S["cw"], b + 1)
                for t in range(NT):
                    y = ps[5 + n % 3][:, t * P:(t + 1) * P]
                    if k < 0:
                        V.tensor_scalar(acc[:, b, t], y, SG[:, b, t:t + 1], None, ALU.mult).then_inc(S["ya"], 1)
                    else:
                        dve.wait_ge(S["ya"], NT * (n - 1) + t + 1)
                        V.scalar_tensor_tensor(out=acc[:, b, t], in0=y, scalar=CW[:, b, t, k:k + 1],
                                               in1=acc[:, b, t], op0=ALU.mult, op1=ALU.add).then_inc(S["ya"], 1)

            def norm_out(b):
                dve.wait_ge(S["ya"], NT * (E + 1) * (b + 1))
                stats(3, b, [acc[:, b, t] for t in range(NT)])

            def finish(b):
                dve.wait_ge(pw[3], b + 1)
                V.tensor_tensor(mh[:, b], MV[:, 3, b, :, 0], RS[:, 3, b], ALU.mult).then_inc(S["mh_s"], 1)
                if b >= 2:
                    dve.wait_ge(stored[b - 2], 16)
                for t in range(NT):
                    V.scalar_tensor_tensor(out=acc[:, b, t], in0=acc[:, b, t], scalar=RS[:, 3, b, t:t + 1],
                                           in1=TR[:, b, t], op0=ALU.mult, op1=ALU.add).then_inc(S["f1"], 1)
                dve.wait_ge(S["mh_s"], b + 1)
                link(V.tensor_tensor(mh[:, b], NM[:, 1, b], mh[:, b], ALU.subtract))
                for t in range(NT):
                    dve.wait_ge(S["f1"], NT * b + t + 1)
                    V.tensor_scalar(FO[:, b % 2, t], acc[:, b, t], mh[:, b, t:t + 1], None,
                                    ALU.add).then_inc(S["f2"], 1)

            for b in range(B):
                n = (E + 2) * b + 1
                dve.wait_ge(S["h"], n + 1)
                dve.wait_ge(S["sh"], (E + 1) * b + 1)
                V.tensor_tensor(hs[:, 3], ps[2 + n % 3][:], hs[:, 3], ALU.mult).then_inc(S["hp"], 1)
                if b == 0:
                    residual(B - 1)
                accumulate(b, -1)
                if b == 0:
                    residual2(B - 1)
                    route2(B - 2)
                accumulate(b, 0)
                if b == 0:
                    neg_mean(2, B - 1)
                if b >= 1:
                    finish(b - 1)
                for k in range(1, E):
                    accumulate(b, k)
                    if b == 0 and k == 5:
                        x3_low(B - 1)
                    if b == 0 and k == 7:
                        route(B - 1)
                if b == 0:
                    route2(B - 1)
                norm_out(b)
            finish(B - 1)


def constants():
    import numpy as np
    c = np.zeros((P, C_END), np.float32)
    eye = np.eye(P, dtype=np.float32)
    c[:, C_ID:C_ID + P] = eye
    for g in range(G):
        for j in (0, 1, 4, 6):
            at = C_SEL + (g * 8 + j) * 32
            c[:, at:at + 32] = eye[:, 32 * g:32 * g + 32]
    p = np.arange(P)
    for h in range(HG):
        c[:MROW, C_HM + h] = (p[:MROW] % 32) // HD == h
    for h in range(H):
        c[MROW:, C_ONE + h] = (p[MROW:] - MROW) % H == h
    for j in range(2):
        half = (p // KEYS == j).astype(np.float32)
        c[:, C_VM + j] = half
        c[:, C_VB + 2 * HD + j] = half
    c[:, C_IO:C_IO + E] = np.arange(E)
    return c


_INS = ["L0_attn_x", "L0_attn_w_qkv", "L0_attn_w_out", "L0_ffn_router_w", "L0_ffn_w1", "L0_ffn_w2",
        "L0_ffn_shared_gate_up", "L0_ffn_shared_down", "L0_ffn_shared_gate_w"]


def kernel(**inputs):
    import numpy as np
    import concourse.bacc as bacc
    from concourse.bass_utils import run_bass_kernel_spmd as run

    nc = bacc.Bacc("TRN2", target_bir_lowering=False, num_devices=1)
    arrays, args = {}, []
    named = [(n, np.ascontiguousarray(inputs[n])) for n in _INS] + [("consts", constants())]
    for n, a in named:
        arrays[f"in_{n}"] = a
        args.append(nc.dram_tensor(f"in_{n}", a.shape, mybir.dt.from_np(a.dtype), kind="ExternalInput").ap())
    out = nc.dram_tensor("out", (B, T, D), F32, kind="ExternalOutput").ap()
    program(nc, *args, out)
    r = run(nc, [arrays], core_ids=[0])
    return r.results[0]["out"]
```

```python
import math
from contextlib import ExitStack

import concourse.bass as bass
from concourse import mybir

F32 = mybir.dt.float32
F32R = mybir.dt.float32r
U32 = mybir.dt.uint32
ACT = mybir.ActivationFunctionType
ALU = mybir.AluOpType
AX = mybir.AxisListType

P = 128
B, T, D = 4, 512, 128
NT = T // P
HT = NT // 2
H, HD = 16, 8
G = 4
HG = H // G
KEYS = 64
KB = NT * KEYS
SNAKE = 23
E = 8
RC = E + 2
VW = 32
QSCALE = float(HD) ** -0.5
EPS = 1e-5
ADDED = 4
TANH = 4
MROW = 96

C_ID, C_SEL = 0, P
C_HM = C_SEL + G * 8 * 32
C_ONE = C_HM + HG
C_VM = C_ONE + G * HG
C_VB = C_VM + 2
C_IO = C_VB + VW
C_END = C_IO + E


def snake_parts():
    rows = T // SNAKE
    return rows - rows % 2, rows * SNAKE


def hidden_bank(n):
    if n == E + 4:
        return 1
    return 4 + n % 2 if n < E + 2 else (2, 4, 3)[(n - E - 2) % 3]


def output_bank(m, tile=0):
    if m == (E + 1) * B - 1 and tile >= HT:
        return 0
    return (3, 0)[m % 2] if m < E + 1 else 5 + (m - E - 1) % 3


def scalar_k(b, k):
    return k in ((-1, 1, 3) if b == B - 1 else (-1, 1, 3, 5))


def weighted(m, tiles=NT):
    b, k = m // (E + 1), m % (E + 1) - 1
    mine = [(c, j) for c in range(B) for j in range(-1, E) if scalar_k(c, j) == scalar_k(b, k)]
    return "yb" if scalar_k(b, k) else "ya", NT * mine.index((b, k)) + tiles


def made(b, k):
    if b == 0:
        return ("sh0", k + 2) if k < TANH else ("sh", k - TANH + 1)
    return "sh", E - TANH + (E + 1) * (b - 1) + k + 2


def program(nc, x, w_qkv, w_out, router_w, w1, w2, gate_up, down, gate_w, consts, out):
    rows, tail = snake_parts()
    with ExitStack() as ctx:
        def sb(name, shape, dt=F32):
            return ctx.enter_context(nc.sbuf_tensor(name, shape, dt))

        def sem(name):
            return ctx.enter_context(nc.semaphore(name))

        cst = sb("cst", [P, C_END])
        sel = sb("sel", [P, G, 8, 32], F32R)
        X = sb("X", [P, B, NT, D])
        XN = sb("XN", [P, 2, NT, D])
        xTh = sb("xTh", [P, T], F32R)
        xTl = sb("xTl", [P, T], F32R)
        wqkv_n = sb("wqkv_n", [P, 3, D])
        wqkvh = sb("wqkvh", [P, 3, D], F32R)
        wqkvl = sb("wqkvl", [P, 3, D], F32R)
        wout_n = sb("wout_n", [P, D])
        woT = sb("woT", [P, D])
        qch = sb("qch", [P, T], F32R)
        qcl = sb("qcl", [P, T], F32R)
        kch = sb("kch", [P, KB], F32R)
        kcl = sb("kcl", [P, KB], F32R)
        xkh = sb("xkh", [P, NT, P], F32R)
        xkl = sb("xkl", [P, NT, P], F32R)
        Qs = sb("Qs", [P, 2, G, T], F32R)
        Ks = sb("Ks", [P, G, KB], F32R)
        Kb = sb("Kb", [P, 2, G, NT, HG, KEYS], F32R)
        Vb = sb("Vb", [P, 2, NT, H // 2, VW])
        AVs = sb("AVs", [P, 2, 2 * P])
        kone = sb("kone", [P, G, HG, KEYS], F32R)
        negm = sb("negm", [P, 2, NT, H])
        Mq = sb("Mq", [P, 2, NT, P], F32R)
        Pr = sb("Pr", [P, 4, 4, P])
        rden = sb("rden", [P, 2, 2, H, 2])
        Y = sb("Y", [P, NT, D])
        O = sb("O", [P, 2, NT, D])
        oT = sb("oT", [P, T])
        TR = sb("TR", [P, B, NT, D])
        X3 = sb("X3", [P, NT, D])
        XH = sb("XH", [P, B, T], F32R)
        XL = sb("XL", [P, B, T], F32R)
        w1n = sb("w1n", [P, E, D])
        w1h = sb("w1h", [P, E, D], F32R)
        w1l = sb("w1l", [P, E, D], F32R)
        w2n = sb("w2n", [P, E, D])
        gun = sb("gun", [P, 2, D])
        guh = sb("guh", [P, 2, D], F32R)
        gul = sb("gul", [P, 2, D], F32R)
        dwn = sb("dwn", [P, D])
        rwn = sb("rwn", [P, RC])
        rwh = sb("rwh", [P, RC], F32R)
        rwl = sb("rwl", [P, RC], F32R)
        hs0 = sb("hs0", [P, 4, T])
        th = XN[:].rearrange("p n t d -> p n (t d)")
        hs = Pr[:].rearrange("p n j q -> p n (j q)")
        acc = X
        Tm = sb("Tm", [P, 3, NT, D])
        FO = XN
        LG = sb("LG", [P, B, NT, RC])
        DL = sb("DL", [P, B, NT, E + 1])
        EX = sb("EX", [P, B, NT, E + 1])
        EZ = sb("EZ", [P, B, NT])
        PB = sb("PB", [P, B, NT, E])
        M8 = sb("M8", [P, B, NT, 8])
        I8 = sb("I8", [P, B, NT, 8], U32)
        EQ = sb("EQ", [P, B, 2, NT, E])
        CW = sb("CW", [P, B, NT, E])
        nmx = sb("nmx", [P, B, 3, NT])
        SG = sb("SG", [P, B, NT])
        mh = sb("mh", [P, B, NT])
        ST = sb("ST", [P, 4, B, NT, 6])
        MV = sb("MV", [P, 4, B, NT, 2])
        VE = sb("VE", [P, 4, B, NT])
        RS = sb("RS", [P, 4, B, NT])
        NM = sb("NM", [P, 4, B, NT])
        nhalf = sb("nhalf", [P, NT])
        warm = sb("warm", [P, 1])
        base = sb("base", [P, NT, E + 1])

        ps = [ctx.enter_context(nc.psum_tensor(f"bank{i}", [P, 512], F32)) for i in range(8)]
        S1, S2 = ps[0:2], ps[2:4]
        PA, PBk = ps[4], ps[5]
        PC, PD = ps[6], ps[7]

        names = ("yz ld_cst ld_wqkv ld_wout ld_w1 ld_w2 ld_gu ld_dwn ld_rw "
                 "selr kones vones mzero nhalf_set base_set wT woT_ps wTh wTl woTr "
                 "w1hs w1ls guhs guls rwhs rwls rwz "
                 "xn xT_ps xh xl qc xk qh ql kc kh kl v_ps vb qs_ps qs_a qs_d ks_ps ks kb_d kb_p "
                 "s1 mx mq mT_ps mev_a mev_d s2 ex pv avc at rd on oT_ps oTs y tr x3n x3T_ps x3h x3l rt lg "
                 "nx dl ez sm pb m8 i8 eq cw sg "
                 "yc h th_s sh0 sh hp ys ya yb pa fa f1 f2 mh_s step").split()
        S = {n: sem(n) for n in names}
        ld_x = [sem(f"ld_x{b}") for b in range(B)]
        st, ag, ve, pw, nm = ([sem(f"{n}{k}") for k in range(4)] for n in ("st", "ag", "ve", "pw", "nm"))
        stored = [sem(f"stored{b}") for b in range(B)]
        ld_id, kdma = sem("ld_id"), sem("kdma")

        ident = cst[:, C_ID:C_ID + P]
        x_v = x.rearrange("b (t p) d -> b p t d", p=P)
        out_v = out.rearrange("b (t p) d -> b p t d", p=P)

        def bank(t, n, w=P):
            return t[:, 0:n * w].rearrange("p (n w) -> p n w", n=n)

        def y_bank(b):
            return PA if b + 1 < B - 1 else S1[0]

        def x3_bank(b):
            return PA if b + 2 < B - 1 else S1[1]

        def s2_bank(n):
            return n % 2 if n < 8 * (B - 1) else 0

        def snake(src, dst):
            s = src[:, 0:rows * SNAKE].rearrange("p (r two c) -> p r two c", two=2, c=SNAKE)
            d = dst[:, 0:rows * SNAKE].rearrange("p (r two c) -> p r two c", two=2, c=SNAKE)
            return [(s[:, :, 0], d[:, :, 0]), (s[:, :, 1, ::-1], d[:, :, 1]), (src[:, tail:T], dst[:, tail:T])]

        def wait_made(engine, b, k):
            name, value = made(b, k)
            engine.wait_ge(S[name], value)

        def wait_weighted(engine, m):
            name, value = weighted(m)
            engine.wait_ge(S[name], value)

        block = ctx.enter_context(nc.Block())

        @block.sync
        def _(sp):
            sp.dma_start(wqkv_n[:], w_qkv.rearrange("(c p) d -> p c d", p=P)).then_inc(S["ld_wqkv"], 16)
            sp.dma_start(X[:, 1], x_v[1]).then_inc(ld_x[1], 16)
            sp.dma_start(cst[:, P:C_END], consts[:, P:C_END]).then_inc(S["ld_cst"], 16)
            sp.dma_start(wout_n[:], w_out).then_inc(S["ld_wout"], 16)
            for b in range(2, B):
                sp.dma_start(X[:, b], x_v[b]).then_inc(ld_x[b], 16)
            sp.dma_start(rwn[:, 0:E], router_w).then_inc(S["ld_rw"], 16)
            sp.dma_start(rwn[:, E:E + 1], gate_w).then_inc(S["ld_rw"], 16)
            sp.dma_start(gun[:], gate_up.rearrange("d (c f) -> d c f", c=2)).then_inc(S["ld_gu"], 16)
            sp.dma_start(w1n[:], w1.rearrange("e d f -> d e f")).then_inc(S["ld_w1"], 16)
            sp.dma_start(w2n[:], w2.rearrange("e f d -> f e d")).then_inc(S["ld_w2"], 16)
            sp.dma_start(dwn[:], down).then_inc(S["ld_dwn"], 16)
            sp.wait_ge(S["kones"], 1)
            for u in range(2):
                for s in range(NT):
                    sp.dma_start(Kb[MROW:P, u, :, s].bitcast(F32), kone[MROW:P].bitcast(F32)).then_inc(kdma, 16)
            for b in range(B - 1):
                sp.wait_ge(S["f2"], NT * (b + 1))
                sp.dma_start(out_v[b], FO[:, b % 2]).then_inc(stored[b], 16)
            for h in range(2):
                sp.wait_ge(S["f2"], NT * (B - 1) + HT * (h + 1))
                sp.dma_start(out_v[B - 1][:, HT * h:HT * (h + 1)],
                             FO[:, (B - 1) % 2, HT * h:HT * (h + 1)]).then_inc(stored[B - 1], 16)
            for b in range(B):
                sp.wait_ge(stored[b], 16 if b < B - 1 else 32)

        @block.gpsimd
        def _(pool):
            nc.gpsimd.memset(nhalf[:], -0.5).then_inc(S["nhalf_set"], 1)
            nc.gpsimd.memset(base[:, :, 0:E], math.e).then_inc(S["base_set"], 1)
            nc.gpsimd.memset(base[:, :, E:E + 1], 1 / math.e).then_inc(S["base_set"], 1)
            nc.gpsimd.memset(rwn[:, E + 1:RC], 0.0).then_inc(S["rwz"], 1)
            nc.gpsimd.memset(Mq[:].bitcast(F32), 0.0).then_inc(S["mzero"], 1)

            def w_low(lo, full, hi, hs_, n, signal):
                pool.wait_ge(hs_, n)
                nc.gpsimd.tensor_tensor(lo, full, hi.bitcast(F32), ALU.subtract).then_inc(signal, 1)

            def k_blocks(b):
                pool.wait_ge(S["ld_cst"], 16)
                pool.wait_ge(S["ks"], 2 * b + 2)
                if b >= 2:
                    pool.wait_ge(S["s2"], 8 * (b - 1))
                shape = [MROW, NT, HG, KEYS]
                for g in (2, 3):
                    rows_ = Ks[0:MROW, g].bitcast(F32).rearrange("p (s k) -> p s k", s=NT)
                    nc.gpsimd.tensor_tensor(
                        Kb[0:MROW, b % 2, g], rows_.unsqueeze(2).to_broadcast(shape),
                        cst[0:MROW, C_HM:C_HM + HG].unsqueeze(1).unsqueeze(3).to_broadcast(shape),
                        ALU.mult).then_inc(S["kb_p"], 1)

            def key_columns(b):
                if b >= 1:
                    pool.wait_ge(S["v_ps"], b)
                for to, src, done in ((xkh, xTh, "xh"), (xkl, xTl, "xl")):
                    pool.wait_ge(S[done], 3 * (b + 1))
                    nc.gpsimd.tensor_copy(
                        to[:].rearrange("p s (two k) -> p s two k", two=2),
                        src[:, 0:T:2].rearrange("p (s k) -> p s k", s=NT).unsqueeze(2)
                        .to_broadcast([P, NT, 2, KEYS])).then_inc(S["xk"], 1)

            def router_exp(b):
                pool.wait_ge(S["base_set"], 2)
                pool.wait_ge(S["dl"], 2 * (b + 1))
                nc.gpsimd.tensor_tensor(EX[:, b], base[:], DL[:, b], ALU.pow).then_inc(S["ez"], 2)

            def powers(k, b):
                pool.wait_ge(ve[k], b + 1)
                if k == 0 and b == 0:
                    pool.wait_ge(S["nhalf_set"], 1)
                nc.gpsimd.tensor_tensor(RS[:, k, b], VE[:, k, b], nhalf[:], ALU.pow).then_inc(pw[k], 1)

            powers(0, 0)
            powers(0, 1)
            key_columns(0)
            k_blocks(0)
            powers(0, 2)
            key_columns(1)
            k_blocks(1)
            powers(0, 3)
            w_low(rwl[:], rwn[:], rwh[:], S["rwhs"], 1, S["rwls"])
            w_low(gul[:], gun[:], guh[:], S["guhs"], 1, S["guls"])

            def add_weighted(b):
                for j in (1, 2) if b < B - 1 else (1,):
                    pool.wait_ge(S["yb"], weighted((E + 1) * b + 2 * j + 2)[1])
                    if j == 2:
                        pool.wait_ge(S["pa"], 2 * b + 1)
                    nc.gpsimd.tensor_tensor(Tm[:, 0], Tm[:, 0], Tm[:, j], ALU.add).then_inc(S["pa"], 1)

            for i in range(B):
                if i >= 1:
                    powers(1, i - 1)
                if i + 2 < B:
                    key_columns(i + 2)
                if i >= 1:
                    powers(2, i - 1)
                if i == B - 1:
                    add_weighted(0)
                if i + 2 < B:
                    k_blocks(i + 2)
                if i == 0:
                    w_low(w1l[:], w1n[:], w1h[:], S["w1hs"], 1, S["w1ls"])
            router_exp(B - 2)
            for b in range(B - 1):
                powers(3, b)
                if b == 0:
                    powers(1, B - 1)
                    powers(2, B - 1)
                if b == 1:
                    router_exp(B - 1)
                add_weighted(b + 1)
            for h in range(2):
                pool.wait_ge(ve[3], B + h)
                nc.gpsimd.tensor_tensor(RS[:, 3, B - 1, HT * h:HT * (h + 1)], VE[:, 3, B - 1, HT * h:HT * (h + 1)],
                                        nhalf[:, 0:HT], ALU.pow).then_inc(pw[3], 1)

        @block.tensor
        def _(pe):
            mm, tp = nc.tensor.matmul, nc.tensor.transpose

            def weights_T():
                pe.wait_ge(ld_id, 16)
                pe.wait_ge(S["ld_wqkv"], 16)
                for c in range(3):
                    i = tp(PC[:, c * P:(c + 1) * P], wqkv_n[:, c], ident)
                i.then_inc(S["wT"], 1)
                pe.wait_ge(S["ld_wout"], 16)
                tp(PD[:, 0:P], wout_n[:], ident).then_inc(S["woT_ps"], 1)

            def warm_up(n, width=T):
                for _ in range(n):
                    mm(S1[0][:, 0:width], Y[:, 0], Y[:].rearrange("p t d -> p (t d)")[:, 0:width], start=True, stop=True)

            def x_T(b):
                if b >= 1:
                    pe.wait_ge(S["qs_a"], 3 * b)
                if b >= 3:
                    pe.wait_ge(S["yc"], b - 2)
                for t in range(NT):
                    pe.wait_ge(S["xn"], NT * b + t + 1)
                    i = tp(PA[:, t * P:(t + 1) * P], XN[:, b % 2, t], ident)
                i.then_inc(S["xT_ps"], 1)

            def split3(out_, wh, wl, vh, vl):
                mm(out_, wh, vh, start=True, stop=False)
                mm(out_, wl, vh, start=False, stop=False)
                return mm(out_, wh, vl, start=False, stop=True)

            def qkv(b):
                pe.wait_ge(S["xh"], 3 * (b + 1))
                pe.wait_ge(S["xl"], 3 * (b + 1))
                if b == 0:
                    pe.wait_ge(S["wTh"], 1)
                    pe.wait_ge(S["wTl"], 1)
                else:
                    pe.wait_ge(S["vb"], 2 * b)
                split3(PBk[:], wqkvh[:, 0], wqkvl[:, 0], xTh[:], xTl[:]).then_inc(S["qc"], 1)
                split3(PA[:, 0:KB], wqkvh[:, 1], wqkvl[:, 1], xTh[:, 0:T:2], xTl[:, 0:T:2]).then_inc(S["kc"], 1)

            def select_k(b):
                if b == 0:
                    pe.wait_ge(S["selr"], 1)
                pe.wait_ge(S["kh"], b + 1)
                pe.wait_ge(S["kl"], b + 1)
                for half in range(2):
                    if half == 1:
                        pe.wait_ge(S["qh"], b + 1)
                        pe.wait_ge(S["ql"], b + 1)
                    for g in (0, 1):
                        o = (PA, PBk)[half][0:MROW, g * KB:(g + 1) * KB]
                        mm(o, sel[:, 2 * half + g, 4:7], kch[:], start=True, stop=False)
                        i = mm(o, sel[:, 2 * half + g, 5:8], kcl[:], start=False, stop=True)
                    i.then_inc(S["ks_ps"], 1)

            def select_q(b, g):
                if g < 2:
                    pe.wait_ge(S["ks"], 2 * b + g + 1)
                else:
                    pe.wait_ge(S["qs_a"], 3 * b + g - 1)
                o = (PA, PBk)[g % 2][0:MROW, :]
                mm(o, sel[:, g, 0:3], qch[:], start=True, stop=False)
                mm(o, sel[:, g, 2:5], qcl[:], start=False, stop=True).then_inc(S["qs_ps"], 1)

            def values(b):
                pe.wait_ge(S["qs_d"], b + 1)
                pe.wait_ge(S["xk"], 2 * b + 2)
                for s in range(NT):
                    o = PBk[:, s * P:(s + 1) * P]
                    mm(o, xkh[:, s], wqkvh[:, 2], start=True, stop=False)
                    mm(o, xkh[:, s], wqkvl[:, 2], start=False, stop=False)
                    i = mm(o, xkl[:, s], wqkvh[:, 2], start=False, stop=True)
                i.then_inc(S["v_ps"], 1)

            def scores_q(b, s, halves=(0, 1)):
                for half in halves:
                    n = (b * NT + s) * 2 + half
                    if half == 0:
                        pe.wait_ge(S["qs_a"], 3 * b + 2)
                        pe.wait_ge(S["kb_d"], HG * (b + 1))
                    else:
                        pe.wait_ge(S["qs_a"], 3 * b + 3)
                        pe.wait_ge(S["qs_d"], b + 1)
                        pe.wait_ge(S["kb_p"], 2 * (b + 1))
                    if n >= 2:
                        pe.wait_ge(S["mx"], n - 1)
                    for j in range(2):
                        g = 2 * half + j
                        i = mm(S1[n % 2][:, j * 256:(j + 1) * 256], Qs[0:MROW, b % 2, g, s * P:(s + 1) * P],
                               Kb[0:MROW, b % 2, g, s], start=True, stop=True)
                    i.then_inc(S["s1"], 1)

            def max_T(b):
                pe.wait_ge(S["mq"], 2 * (b + 1))
                if b >= 1:
                    pe.wait_ge(S["avc"], NT * b)
                for s in range(NT):
                    i = tp(PC[:, s * P:(s + 1) * P], Mq[:, b % 2, s].bitcast(F32), ident)
                i.then_inc(S["mT_ps"], 1)

            def scores_k(b, s, halves=(0, 1)):
                for half in halves:
                    n = (b * NT + s) * 2 + half
                    pe.wait_ge(*((S["mev_d"], b + 1) if half else (S["mev_a"], 2 * b + 2)))
                    if b == 0 and s == 0 and half == 0:
                        pe.wait_ge(kdma, 16 * 2 * NT)
                    if n >= 2:
                        pe.wait_ge(S["ex"], n if b == B - 1 else n - 1)
                    for j in range(4):
                        g, pr = 2 * half + j // 2, j % 2
                        i = mm(S2[s2_bank(n)][:, j * P:(j + 1) * P],
                               Kb[:, b % 2, g, s, 2 * pr:2 * pr + 2],
                               Qs[:, b % 2, g, s * P:(s + 1) * P], start=True, stop=True)
                    i.then_inc(S["s2"], 1)

            def attend(b, s):
                if s == 0:
                    pe.wait_ge(S["mev_a"], 2 * b + 2)
                if NT * b + s >= 1:
                    pe.wait_ge(S["avc"], NT * b + s)
                pe.wait_ge(S["vb"], 2 * (b + 1))
                pe.wait_ge(S["vones"], 2)
                for half in range(2):
                    n = (b * NT + s) * 2 + half
                    pe.wait_ge(S["ex"], n + 1)
                    for j in range(4):
                        i = mm(PC[j * VW:(j + 1) * VW, (s % 2) * 2 * P + half * P:(s % 2) * 2 * P + (half + 1) * P],
                               Vb[:, b % 2, s, half * 4 + j], Pr[:, n % 4, j], start=True, stop=True)
                i.then_inc(S["pv"], 1)

            def attend_T(b, s):
                pe.wait_ge(S["avc"], NT * b + s + 1)
                if s == 0 and b >= 1:
                    pe.wait_ge(S["oTs"], b)
                if s == 2:
                    pe.wait_ge(S["on"], 2 * b + 1)
                for half in range(2):
                    c = (s % 2) * 2 * P + half * P
                    i = tp(PD[:, c:c + P], AVs[:, s % 2, half * P:(half + 1) * P], ident)
                i.then_inc(S["at"], 1)

            def output_T(b):
                pe.wait_ge(S["on"], 2 * (b + 1))
                for s in range(NT):
                    i = tp(PD[:, s * P:(s + 1) * P], O[:, b % 2, s], ident)
                i.then_inc(S["oT_ps"], 1)

            def project(b):
                pe.wait_ge(S["oTs"], b + 1)
                if b == 0:
                    pe.wait_ge(S["woTr"], 1)
                if b < B - 2:
                    pe.wait_ge(S["qs_a"], 3 * (b + 3))
                elif b < B - 1:
                    pe.wait_ge(S["mx"], 8 * B)
                else:
                    wait_weighted(pe, E - 1)
                for s in range(NT):
                    i = mm(y_bank(b)[:, s * P:(s + 1) * P], oT[:, s * P:(s + 1) * P], woT[:], start=True, stop=True)
                i.then_inc(S["y"], 1)

            def moe_in(b):
                pe.wait_ge(S["x3n"], NT * (b + 1))
                if b < B - 3:
                    pe.wait_ge(S["yc"], b + 2)
                else:
                    pe.wait_ge(S["mx"], 8 * B)
                if b == B - 1:
                    wait_made(pe, 1, 0)
                for s in range(NT):
                    i = tp(x3_bank(b)[:, s * P:(s + 1) * P], X3[:, s], ident)
                i.then_inc(S["x3T_ps"], 1)

            def router(b):
                pe.wait_ge(S["x3h"], b + 1)
                pe.wait_ge(S["x3l"], b + 1)
                pe.wait_ge(S["rwhs"], 1)
                pe.wait_ge(S["rwls"], 1)
                for s in range(NT):
                    xh, xl = XH[:, b, s * P:(s + 1) * P], XL[:, b, s * P:(s + 1) * P]
                    o = x3_bank(b)[:, s * RC:(s + 1) * RC]
                    mm(o, xh, rwh[:], start=True, stop=False)
                    mm(o, xh, rwl[:], start=False, stop=False)
                    i = mm(o, xl, rwh[:], start=False, stop=True)
                i.then_inc(S["rt"], 1)

            pe.wait_ge(S["yz"], 1)
            warm_up(2)
            weights_T()
            warm_up(1, 256)
            x_T(0)
            warm_up(1)
            qkv(0)
            select_k(0)
            for g in range(G):
                select_q(0, g)
            scores_q(0, 0, (0,))
            values(0)
            scores_q(0, 0, (1,))
            x_T(1)
            scores_q(0, 1)
            qkv(1)
            scores_q(0, 2)
            select_k(1)
            scores_q(0, 3)
            for i in range(B - 1):
                p1 = i + 2 < B
                select_q(i + 1, 0)
                max_T(i)
                select_q(i + 1, 1)
                if i >= 1:
                    output_T(i - 1)
                select_q(i + 1, 2)
                select_q(i + 1, 3)
                scores_k(i, 0)
                scores_q(i + 1, 0)
                if i >= 1:
                    project(i - 1)
                scores_k(i, 1)
                attend(i, 0)
                scores_q(i + 1, 1)
                if i >= 2:
                    moe_in(i - 2)
                values(i + 1)
                if p1:
                    x_T(i + 2)
                scores_k(i, 2)
                attend_T(i, 0)
                attend(i, 1)
                scores_q(i + 1, 2)
                if i >= 2:
                    router(i - 2)
                if p1:
                    qkv(i + 2)
                scores_k(i, 3)
                attend_T(i, 1)
                attend(i, 2)
                scores_q(i + 1, 3)
                if p1:
                    select_k(i + 2)
                attend_T(i, 2)
                attend(i, 3)
                attend_T(i, 3)

            def hidden(n, wh, wl, b):
                if b == 0:
                    if n == 0:
                        pe.wait_ge(S["vb"], 2 * B)
                        pe.wait_ge(S["qs_a"], 3 * B)
                        pe.wait_ge(S["yc"], B - 2)
                        pe.wait_ge(S["lg"], B - 3)
                    elif n == 3:
                        pe.wait_ge(S["hp"], 1)
                    elif n >= 2:
                        wait_made(pe, 0, max(n - 4, -1))
                elif n < E + 5:
                    if n == E + 2:
                        pe.wait_ge(S["ex"], 8 * B)
                    elif n == E + 3:
                        wait_made(pe, 0, E - 2)
                    else:
                        pe.wait_ge(S["lg"], B - 1)
                elif n == E + 7:
                    wait_weighted(pe, E)
                else:
                    c, m = divmod(n - 3, E + 2)
                    if m == 1:
                        pe.wait_ge(S["hp"], c + 1)
                    else:
                        wait_made(pe, c, max(m - 2, -1))
                split3(ps[hidden_bank(n)][:], wh, wl, XH[:, b], XL[:, b]).then_inc(S["h"], 1)

            def outputs(n, lhs, w):
                if n < E + 1:
                    if n == 0:
                        pe.wait_ge(S["ex"], 8 * (B - 1))
                    elif n == 1:
                        pe.wait_ge(S["yc"], B - 1)
                    else:
                        wait_weighted(pe, n - 2)
                elif n < E + 4:
                    pe.wait_ge(*((S["sh"], made(0, E - 1)[1]), (S["avc"], NT * B), (S["oTs"], B))[n - E - 1])
                else:
                    wait_weighted(pe, n - 3)
                if n == (E + 1) * B - 1:
                    pe.wait_ge(S["yc"], B)
                for s in range(NT):
                    i = mm(ps[output_bank(n, s)][:, s * P:(s + 1) * P], lhs[:, s * P:(s + 1) * P], w,
                           start=True, stop=True)
                    if n == (E + 1) * B - 1 and s == HT - 1:
                        i.then_inc(S["ys"], 1)
                i.then_inc(S["ys"], 1)

            def gate(b):
                hidden((E + 2) * b, guh[:, 0], gul[:, 0], b)

            def up(b):
                hidden((E + 2) * b + 1, guh[:, 1], gul[:, 1], b)

            def expert_h(b, e):
                hidden((E + 2) * b + 2 + e, w1h[:, e], w1l[:, e], b)

            def shared_o(b):
                pe.wait_ge(S["hp"], b + 1)
                outputs((E + 1) * b, (hs0 if b == 0 else hs)[:, 3], dwn[:])

            def expert_o(b, e):
                wait_made(pe, b, e)
                outputs((E + 1) * b + 1 + e, (hs0 if b == 0 else hs)[:, e % 3], w2n[:, e])

            i = B - 1
            for n_ in ("w1hs", "w1ls", "guhs", "guls"):
                pe.wait_ge(S[n_], 1)
            pe.wait_ge(S["ld_w2"], 16)
            pe.wait_ge(S["ld_dwn"], 16)
            max_T(i)
            gate(0)
            output_T(i - 1)
            moe_in(i - 2)
            scores_k(i, 0, (0,))
            up(0)
            project(i - 1)
            scores_k(i, 0, (1,))
            expert_h(0, 0)
            scores_k(i, 1, (0,))
            shared_o(0)
            scores_k(i, 1, (1,))
            expert_h(0, 1)
            attend(i, 0)
            router(i - 2)
            scores_k(i, 2, (0,))
            expert_o(0, 0)
            scores_k(i, 2, (1,))
            expert_h(0, 2)
            attend_T(i, 0)
            attend(i, 1)
            scores_k(i, 3, (0,))
            expert_o(0, 1)
            scores_k(i, 3, (1,))
            expert_h(0, 3)
            attend_T(i, 1)
            attend(i, 2)
            expert_o(0, 2)
            attend_T(i, 2)
            attend(i, 3)
            expert_h(0, 4)
            attend_T(i, 3)
            expert_o(0, 3)
            expert_h(0, 5)
            expert_o(0, 4)
            output_T(i)
            expert_h(0, 6)
            moe_in(i - 1)
            expert_o(0, 5)
            expert_h(0, 7)
            router(i - 1)
            expert_o(0, 6)
            gate(1)
            up(1)
            expert_o(0, 7)

            for b in range(1, B):
                if b == 1:
                    project(B - 1)
                expert_h(b, 0)
                shared_o(b)
                for e in range(E):
                    if e + 1 < E:
                        expert_h(b, e + 1)
                    elif b + 1 < B:
                        gate(b + 1)
                        up(b + 1)
                    expert_o(b, e)
                    if b == 1 and e == 6:
                        moe_in(B - 1)
                    if b == 1 and e == 7:
                        router(B - 1)

        @block.scalar
        def _(act):
            A = nc.scalar.activation
            act.dma_start(X[:, 0], x_v[0]).then_inc(ld_x[0], 16)
            act.dma_start(cst[:, 0:P], consts[:, 0:P]).then_inc(ld_id, 16)

            def normalise_x(b):
                act.wait_ge(nm[0], b + 1)
                act.wait_ge(ld_x[b], 16)
                if b >= 2:
                    act.wait_ge(S["xT_ps"], b - 1)
                for t in range(NT):
                    A(XN[:, b % 2, t], X[:, b, t], ACT.Identity, scale=RS[:, 0, b, t:t + 1],
                      bias=NM[:, 0, b, t:t + 1]).then_inc(S["xn"], 1)

            def x_high(b):
                act.wait_ge(S["xT_ps"], b + 1)
                if b >= 1:
                    act.wait_ge(S["kc"], b)
                    act.wait_ge(S["xk"], 2 * b)
                for s_, d_ in snake(PA, xTh):
                    A(d_, s_, ACT.Copy).then_inc(S["xh"], 1)

            def max_rows(b):
                act.wait_ge(S["mT_ps"], b + 1)
                if b >= 2:
                    act.wait_ge(S["s2"], 8 * (b - 1))
                for g in range(2):
                    A(Qs[MROW:P, b % 2, g], PC[MROW:P, 0:T], ACT.Copy).then_inc(S["mev_a"], 1)

            def qk_high(b):
                act.wait_ge(S["qc"], b + 1)
                if b >= 1:
                    act.wait_ge(S["qs_ps"], G * b)
                A(qch[:], PBk[:], ACT.Copy, scale=QSCALE).then_inc(S["qh"], 1)
                act.wait_ge(S["kc"], b + 1)
                if b >= 1:
                    act.wait_ge(S["ks_ps"], 2 * b)
                A(kch[:], PA[:, 0:KB], ACT.Copy).then_inc(S["kh"], 1)

            def o_copy(b):
                act.wait_ge(S["oT_ps"], b + 1)
                if b >= 1:
                    act.wait_ge(S["y"], b)
                A(oT[:], PD[:], ACT.Copy).then_inc(S["oTs"], 1)

            def y_copy(b):
                act.wait_ge(S["y"], b + 1)
                if b >= 1:
                    act.wait_ge(S["tr"], NT * b)
                A(Y[:], bank(y_bank(b), NT), ACT.Copy).then_inc(S["yc"], 1)

            def q_rows(b, g):
                if b >= 2:
                    act.wait_ge(S["s2"], 8 * (b - 1))
                act.wait_ge(S["qs_ps"], G * b + g + 1)
                A(Qs[0:MROW, b % 2, g], (PA, PBk)[g % 2][0:MROW, :], ACT.Copy).then_inc(S["qs_a"], 1)

            def k_rows(b, half):
                act.wait_ge(S["ks_ps"], 2 * b + half + 1)
                if b >= 1:
                    act.wait_ge(*((S["kb_d"], HG * b) if half == 0 else (S["kb_p"], 2 * b)))
                A(Ks[0:MROW, 2 * half:2 * half + 2], (PA, PBk)[half][0:MROW, :].rearrange(
                    "p (g n) -> p g n", g=2), ACT.Copy).then_inc(S["ks"], 1)

            def v_blocks(b):
                act.wait_ge(S["v_ps"], b + 1)
                if b == 0:
                    act.wait_ge(S["vones"], 2)
                if b >= 2:
                    act.wait_ge(S["pv"], NT * (b - 1))
                v = PBk[:].rearrange("p (j two c) -> p j two c", two=2, c=HD)
                o = Vb[:, b % 2].rearrange("p s j c -> p (s j) c")
                for j in range(2):
                    A(o[:, :, j * HD:(j + 1) * HD], v[:, :, j], ACT.Copy,
                      scale=cst[:, C_VM + j:C_VM + j + 1]).then_inc(S["vb"], 1)

            def attended(b, s):
                n = NT * b + s
                act.wait_ge(S["pv"], n + 1)
                if n >= 2:
                    act.wait_ge(S["at"], n - 1)
                A(AVs[:, s % 2], PC[:, (s % 2) * 2 * P:(s % 2 + 1) * 2 * P], ACT.Copy).then_inc(S["avc"], 1)

            def exps(b, s, halves=(0, 1)):
                for half in halves:
                    n = (b * NT + s) * 2 + half
                    act.wait_ge(S["s2"], n + 1)
                    if n >= 4:
                        act.wait_ge(S["pv"], (n - 4) // 2 + 1)
                    A(Pr[:, n % 4], bank(S2[s2_bank(n)], 4), ACT.Exp).then_inc(S["ex"], 1)

            def normalise_3(b, tiles=range(NT)):
                act.wait_ge(nm[2], b + 1)
                if b >= 1:
                    act.wait_ge(S["x3T_ps"], b)
                for t in tiles:
                    A(X3[:, t], TR[:, b, t], ACT.Identity, scale=RS[:, 2, b, t:t + 1],
                      bias=NM[:, 2, b, t:t + 1]).then_inc(S["x3n"], 1)

            def x3_high(b):
                act.wait_ge(S["x3T_ps"], b + 1)
                A(XH[:, b], x3_bank(b)[:], ACT.Copy).then_inc(S["x3h"], 1)

            def router_exp(b):
                act.wait_ge(S["dl"], 2 * (b + 1))
                A(EX[:, b, :, 0:E], DL[:, b, :, 0:E], ACT.Exp).then_inc(S["ez"], 1)
                A(EX[:, b, :, E:E + 1], DL[:, b, :, E:E + 1], ACT.Exp, scale=-1.0).then_inc(S["ez"], 1)

            act.wait_ge(S["nhalf_set"], 1)
            A(warm[:], nhalf[:, 0:1], ACT.Exp)
            normalise_x(0)
            act.wait_ge(S["wT"], 1)
            A(wqkvh[:], bank(PC, 3), ACT.Copy).then_inc(S["wTh"], 1)
            x_high(0)
            act.wait_ge(S["woT_ps"], 1)
            A(woT[:], PD[:, 0:P], ACT.Copy).then_inc(S["woTr"], 1)
            act.wait_ge(S["ld_cst"], 16)
            A(kone[MROW:P], cst[MROW:P, C_ONE:C_ONE + G * HG].rearrange("p (g h) -> p g h", g=G).unsqueeze(3)
              .to_broadcast([P - MROW, G, HG, KEYS]), ACT.Copy).then_inc(S["kones"], 1)
            qk_high(0)
            k_rows(0, 0)
            k_rows(0, 1)
            for g in range(G - 1):
                q_rows(0, g)
            normalise_x(1)
            v_blocks(0)
            x_high(1)
            act.wait_ge(S["ld_rw"], 32)
            act.wait_ge(S["rwz"], 1)
            A(rwh[:], rwn[:], ACT.Copy).then_inc(S["rwhs"], 1)
            act.wait_ge(S["ld_gu"], 16)
            A(guh[:], gun[:], ACT.Copy).then_inc(S["guhs"], 1)
            qk_high(1)
            k_rows(1, 0)
            k_rows(1, 1)
            act.wait_ge(S["ld_w1"], 16)
            A(w1h[:], w1n[:], ACT.Copy).then_inc(S["w1hs"], 1)
            normalise_x(2)
            for i in range(B - 1):
                p1 = i + 2 < B
                q_rows(i + 1, 0)
                max_rows(i)
                for g in range(1, G - 1):
                    q_rows(i + 1, g)
                if i >= 1:
                    o_copy(i - 1)
                exps(i, 0)
                if i >= 1:
                    y_copy(i - 1)
                exps(i, 1)
                attended(i, 0)
                if i >= 2:
                    x3_high(i - 2)
                if i + 3 < B:
                    normalise_x(i + 3)
                v_blocks(i + 1)
                if p1:
                    x_high(i + 2)
                exps(i, 2)
                attended(i, 1)
                exps(i, 3)
                if p1:
                    qk_high(i + 2)
                attended(i, 2)
                if p1:
                    k_rows(i + 2, 0)
                    k_rows(i + 2, 1)
                attended(i, 3)
                if i >= 1:
                    normalise_3(i - 1)
                if i >= 2:
                    router_exp(i - 2)

            def tanh(k):
                n, m = (0, 0) if k < 0 else (k + 2, k + 1)
                act.wait_ge(S["h"], n + 1)
                if m == 0:
                    act.wait_ge(S["s2"], 8 * (B - 1))
                if m >= 2:
                    act.wait_ge(S["sh0"], m - 1)
                A(th[:, m % 2], ps[hidden_bank(n)][:], ACT.Tanh, scale=0.5).then_inc(S["th_s"], 1)

            def silu(b, k):
                n = (E + 2) * b + (0 if k < 0 else k + 2)
                act.wait_ge(S["h"], n + 1)
                if b == 1 and k < 3:
                    act.wait_ge(S["pv"], NT * B)
                elif b == 0:
                    act.wait_ge(S["ys"], k - 1)
                elif k < 0:
                    act.wait_ge(S["ys"], (E + 1) * (b - 1) + 1)
                elif k >= 3:
                    act.wait_ge(S["ys"], (E + 1) * b + k - 1)
                else:
                    last = max(e for e in range(E) if e % 3 == k)
                    act.wait_ge(S["ys"], (E + 1) * (b - 1) + last + 2)
                A((hs0 if b == 0 else hs)[:, k % 3 if k >= 0 else 3], ps[hidden_bank(n)][:],
                  ACT.Silu).then_inc(S["sh"], 1)

            def weight(b, k):
                n = (E + 1) * b + k + 1
                act.wait_ge(S["ys"], n + 1)
                if k < 0:
                    act.wait_ge(S["sg"], b + 1)
                    act.wait_ge(S["tr"], NT * (b + 1))
                else:
                    act.wait_ge(S["cw"], b + 2)
                    if b >= 1:
                        act.wait_ge(S["fa"], b)
                for t in range(NT):
                    A(acc[:, b, t] if k < 0 else Tm[:, k // 2, t], ps[output_bank(n)][:, t * P:(t + 1) * P], ACT.Copy,
                      scale=SG[:, b, t:t + 1] if k < 0 else CW[:, b, t, k:k + 1]).then_inc(S["yb"], 1)

            def finish_out(b, t0=0, t1=NT):
                act.wait_ge(S["mh_s"], 2 * (b + 1) + (2 if t0 else 0))
                if b >= 2:
                    act.wait_ge(stored[b - 2], 16)
                for t in range(t0, t1):
                    act.wait_ge(S["f1"], NT * b + t + 1)
                    A(FO[:, b % 2, t], acc[:, b, t], ACT.Identity, bias=mh[:, b, t:t + 1]).then_inc(S["f2"], 1)

            i = B - 1
            max_rows(i)
            tanh(-1)
            o_copy(i - 1)
            exps(i, 0, (0,))
            x3_high(i - 2)
            y_copy(i - 1)
            exps(i, 0, (1,))
            tanh(0)
            exps(i, 1)
            tanh(1)
            weight(0, -1)
            attended(i, 0)
            exps(i, 2)
            tanh(2)
            attended(i, 1)
            router_exp(i - 2)
            exps(i, 3)
            tanh(3)
            weight(0, 1)
            attended(i, 2)
            normalise_3(i - 1, (0, 1, 2))
            attended(i, 3)
            silu(0, 4)
            weight(0, 3)
            silu(0, 5)
            normalise_3(i - 1, (3,))
            o_copy(i)
            silu(0, 6)
            x3_high(i - 1)
            weight(0, 5)
            silu(0, 7)

            for b in range(1, B):
                silu(b, -1)
                if b == 1:
                    y_copy(B - 1)
                silu(b, 0)
                weight(b, -1)
                for k in range(1, E):
                    silu(b, k)
                    if k % 2 == 0 and scalar_k(b, k - 1):
                        weight(b, k - 1)
                    if b == B - 1 and k == 5:
                        finish_out(b - 1)
                    if b == 1 and k in (5, 6):
                        normalise_3(B - 1, (2 * (k - 5), 2 * (k - 5) + 1))
                    if b == 1 and k == 7:
                        x3_high(B - 1)
                if b < B - 1:
                    finish_out(b - 1)
            finish_out(B - 1, 0, HT)
            finish_out(B - 1, HT, NT)

        @block.vector
        def _(dve):
            V = nc.vector
            steps = [0]

            def link(ins):
                steps[0] += 1
                ins.then_inc(S["step"], 1)
                dve.wait_ge(S["step"], steps[0])

            def stats(k, b, tiles, t0=0, t1=NT):
                for t in range(t0, t1):
                    V.bn_stats(ST[:, k, b, t], tiles[t]).then_inc(st[k], 1)
                for t in range(t0, t1):
                    dve.wait_ge(st[k], NT * b + t + 1)
                    V.bn_aggr(MV[:, k, b, t], ST[:, k, b, t]).then_inc(ag[k], 1)
                dve.wait_ge(ag[k], NT * b + t1)
                V.tensor_scalar(VE[:, k, b, t0:t1], MV[:, k, b, t0:t1, 1], EPS, None, ALU.add).then_inc(ve[k], 1)

            def neg_mean(k, b):
                dve.wait_ge(pw[k], b + 1)
                V.scalar_tensor_tensor(out=NM[:, k, b], in0=MV[:, k, b, :, 0], scalar=-1.0, in1=RS[:, k, b],
                                       op0=ALU.mult, op1=ALU.mult).then_inc(nm[k], 1)

            def stats_x(b):
                dve.wait_ge(ld_x[b], 16)
                stats(0, b, [X[:, b, t] for t in range(NT)])

            def x_low(b):
                dve.wait_ge(S["xh"], 3 * (b + 1))
                if b >= 1:
                    dve.wait_ge(S["kc"], b)
                    dve.wait_ge(S["xk"], 2 * b)
                for (s_, d_), (_, h_) in zip(snake(PA, xTl), snake(PA, xTh)):
                    V.tensor_tensor(d_, s_, h_.bitcast(F32), ALU.subtract).then_inc(S["xl"], 1)

            def qk_low(b):
                dve.wait_ge(S["qh"], b + 1)
                V.scalar_tensor_tensor(out=qcl[:], in0=PBk[:], scalar=QSCALE, in1=qch[:].bitcast(F32),
                                       op0=ALU.mult, op1=ALU.subtract).then_inc(S["ql"], 1)
                dve.wait_ge(S["kh"], b + 1)
                V.tensor_tensor(kcl[:], PA[:, 0:KB], kch[:].bitcast(F32), ALU.subtract).then_inc(S["kl"], 1)

            def k_blocks(b):
                dve.wait_ge(S["ks"], 2 * b + 1)
                if b >= 2:
                    dve.wait_ge(S["s2"], 8 * (b - 1))
                for h in range(HG):
                    V.tensor_scalar(Kb[0:MROW, b % 2, 0:2, :, h].rearrange("p g s k -> p (g s) k"),
                                    Ks[0:MROW, 0:2].bitcast(F32).rearrange("p g (s k) -> p (g s) k", k=KEYS),
                                    cst[0:MROW, C_HM + h:C_HM + h + 1], None, ALU.mult).then_inc(S["kb_d"], 1)

            def max_rows(b):
                dve.wait_ge(S["mev_a"], 2 * b + 1)
                if b >= 2:
                    dve.wait_ge(S["s2"], 8 * (b - 1))
                V.tensor_copy(Qs[MROW:P, b % 2, 2:4], Qs[MROW:P, b % 2, 0:1].bitcast(F32)
                              .to_broadcast([P - MROW, 2, T])).then_inc(S["mev_d"], 1)

            def q_rows(b):
                if b >= 2:
                    dve.wait_ge(S["s2"], 8 * (b - 1))
                dve.wait_ge(S["qs_ps"], G * b + G)
                V.tensor_copy(Qs[0:MROW, b % 2, G - 1], PBk[0:MROW, :]).then_inc(S["qs_d"], 1)

            def maxima(b, s):
                for half in range(2):
                    n = (b * NT + s) * 2 + half
                    dve.wait_ge(S["s1"], n + 1)
                    V.tensor_reduce(negm[:, b % 2, s, 8 * half:8 * half + 8], bank(S1[n % 2], 8, KEYS), AX.X,
                                    ALU.max, negate=True).then_inc(S["mx"], 1)

            def max_split(b):
                dve.wait_ge(S["mx"], 8 * (b + 1))
                if b == 0:
                    dve.wait_ge(S["mzero"], 1)
                V.tensor_copy(Mq[:, b % 2, :, MROW:MROW + H], negm[:, b % 2]).then_inc(S["mq"], 1)
                dve.wait_ge(S["mq"], 2 * b + 1)
                V.tensor_tensor(Mq[:, b % 2, :, MROW + H:P], negm[:, b % 2],
                                Mq[:, b % 2, :, MROW:MROW + H].bitcast(F32), ALU.subtract).then_inc(S["mq"], 1)

            def divide(b, c):
                dve.wait_ge(S["at"], NT * b + 2 * c + 2)
                o = PD[:].rearrange("p (j w) -> p j w", w=VW)
                V.reciprocal(rden[:, b % 2, c], o[:, :, 2 * HD:2 * HD + 2]).then_inc(S["rd"], 1)
                dve.wait_ge(S["rd"], 2 * b + c + 1)
                V.tensor_tensor(O[:, b % 2, 2 * c:2 * c + 2].rearrange("p s (j two d) -> p (s j) two d", two=2, d=HD),
                                o[:, :, 0:2 * HD].rearrange("p j (two d) -> p j two d", two=2),
                                rden[:, b % 2, c].unsqueeze(3).to_broadcast([P, H, 2, HD]),
                                ALU.mult).then_inc(S["on"], 1)

            def residual(b):
                dve.wait_ge(S["yc"], b + 1)
                stats(1, b, [Y[:, t] for t in range(NT)])

            def residual2(b):
                neg_mean(1, b)
                for t in range(NT):
                    V.scalar_tensor_tensor(out=TR[:, b, t], in0=Y[:, t], scalar=RS[:, 1, b, t:t + 1],
                                           in1=X[:, b, t], op0=ALU.mult, op1=ALU.add).then_inc(S["tr"], 1)
                dve.wait_ge(S["tr"], NT * (b + 1))
                stats(2, b, [TR[:, b, t] for t in range(NT)])

            def x3_low(b):
                dve.wait_ge(S["x3h"], b + 1)
                V.tensor_tensor(XL[:, b], x3_bank(b)[:], XH[:, b].bitcast(F32), ALU.subtract).then_inc(S["x3l"], 1)

            def route(b):
                dve.wait_ge(S["rt"], b + 1)
                V.tensor_copy(LG[:, b], bank(x3_bank(b), NT, RC)).then_inc(S["lg"], 1)
                dve.wait_ge(S["lg"], b + 1)
                V.tensor_reduce(nmx[:, b, 0], LG[:, b, :, 0:E], AX.X, ALU.max, negate=True).then_inc(S["nx"], 1)
                dve.wait_ge(S["nx"], b + 1)
                V.tensor_tensor(DL[:, b, :, 0:E], LG[:, b, :, 0:E], nmx[:, b, 0].unsqueeze(2).to_broadcast([P, NT, E]),
                                ALU.add).then_inc(S["dl"], 1)
                V.tensor_copy(DL[:, b, :, E:E + 1], LG[:, b, :, E:E + 1]).then_inc(S["dl"], 1)

            def route2(b):
                def wide(a):
                    return a.unsqueeze(2).to_broadcast([P, NT, E])

                dve.wait_ge(S["ez"], 2 * (b + 1))
                V.tensor_scalar(EZ[:, b], EX[:, b, :, E], 1.0, None, ALU.add).then_inc(S["sm"], 1)
                link(V.tensor_reduce(nmx[:, b, 1], EX[:, b, :, 0:E], AX.X, ALU.add))
                dve.wait_ge(S["sm"], b + 1)
                V.reciprocal(SG[:, b], EZ[:, b]).then_inc(S["sg"], 1)
                link(V.reciprocal(nmx[:, b, 2], nmx[:, b, 1]))
                V.tensor_tensor(PB[:, b], EX[:, b, :, 0:E], wide(nmx[:, b, 2]), ALU.mult).then_inc(S["pb"], 1)
                dve.wait_ge(S["pb"], b + 1)
                for t in range(NT):
                    V.max(M8[:, b, t], PB[:, b, t]).then_inc(S["m8"], 1)
                for t in range(NT):
                    dve.wait_ge(S["m8"], NT * b + t + 1)
                    V.max_index(I8[:, b, t], M8[:, b, t], PB[:, b, t]).then_inc(S["i8"], 1)
                dve.wait_ge(S["i8"], NT * (b + 1))
                iota = cst[:, C_IO:C_IO + E].unsqueeze(1).to_broadcast([P, NT, E])
                for j in range(2):
                    V.tensor_tensor(EQ[:, b, j], iota, wide(I8[:, b, :, j]), ALU.is_equal).then_inc(S["eq"], 1)
                dve.wait_ge(S["eq"], 2 * (b + 1))
                link(V.tensor_tensor(EQ[:, b, 0], EQ[:, b, 0], EQ[:, b, 1], ALU.add))
                half = TANH if b == 0 else 0
                for e0, e1, c in ((0, half, 0.5), (half, E, 1.0)):
                    if e1 > e0:
                        V.scalar_tensor_tensor(out=CW[:, b, :, e0:e1], in0=EQ[:, b, 0, :, e0:e1], scalar=c,
                                               in1=PB[:, b, :, e0:e1], op0=ALU.mult, op1=ALU.mult).then_inc(S["cw"], 1)

            V.memset(Y[:], 0.0).then_inc(S["yz"], 1)
            stats_x(0)
            neg_mean(0, 0)
            stats_x(1)
            dve.wait_ge(S["wTh"], 1)
            V.tensor_tensor(wqkvl[:], bank(PC, 3), wqkvh[:].bitcast(F32), ALU.subtract).then_inc(S["wTl"], 1)
            x_low(0)
            neg_mean(0, 1)
            dve.wait_ge(S["ld_cst"], 16)
            V.tensor_copy(sel[:].rearrange("p g b c -> p (g b c)"), cst[:, C_SEL:C_HM]).then_inc(S["selr"], 1)
            qk_low(0)
            for u in range(2):
                V.tensor_copy(Vb[:, u].rearrange("p s j c -> p (s j) c"), cst[:, C_VB:C_VB + VW].unsqueeze(1)
                              .to_broadcast([P, NT * H // 2, VW])).then_inc(S["vones"], 1)
            k_blocks(0)
            stats_x(2)
            q_rows(0)
            maxima(0, 0)
            neg_mean(0, 2)
            x_low(1)
            maxima(0, 1)
            qk_low(1)
            maxima(0, 2)
            stats_x(3)
            maxima(0, 3)
            max_split(0)
            k_blocks(1)
            neg_mean(0, 3)
            for i in range(B - 1):
                p1 = i + 2 < B
                max_rows(i)
                q_rows(i + 1)
                maxima(i + 1, 0)
                maxima(i + 1, 1)
                if i >= 1:
                    residual(i - 1)
                if i >= 2:
                    x3_low(i - 2)
                if p1:
                    x_low(i + 2)
                maxima(i + 1, 2)
                if i >= 1:
                    residual2(i - 1)
                if p1:
                    qk_low(i + 2)
                divide(i, 0)
                if i >= 2:
                    route(i - 2)
                if i >= 1:
                    neg_mean(2, i - 1)
                maxima(i + 1, 3)
                max_split(i + 1)
                if p1:
                    k_blocks(i + 2)
                divide(i, 1)

            def accumulate(b, k):
                n = (E + 1) * b + k + 1
                dve.wait_ge(S["ys"], n + 1)
                if k == 0:
                    dve.wait_ge(S["cw"], b + 2)
                if b == B - 1 and k == ADDED + 1:
                    dve.wait_ge(S["fa"], B)
                before = max(j for j in range(-1, k) if j < 0 or not scalar_k(b, j))
                for t in range(NT):
                    name, value = weighted(n - k + before, t + 1)
                    dve.wait_ge(S[name], value)
                    V.scalar_tensor_tensor(out=acc[:, b, t], in0=ps[output_bank(n)][:, t * P:(t + 1) * P],
                                           scalar=CW[:, b, t, k:k + 1], in1=acc[:, b, t],
                                           op0=ALU.mult, op1=ALU.add).then_inc(S["ya"], 1)

            def add_other(b):
                dve.wait_ge(S["pa"], 2 * (b + 1) - (b == B - 1))
                dve.wait_ge(S["ya"], weighted((E + 1) * b + (ADDED if b == B - 1 else E - 1) + 1)[1])
                V.tensor_tensor(acc[:, b], acc[:, b], Tm[:, 0], ALU.add).then_inc(S["fa"], 1)

            def norm_out(b):
                dve.wait_ge(S["ya"], weighted((E + 1) * b + E)[1])
                dve.wait_ge(S["fa"], b + 1)
                stats(3, b, [acc[:, b, t] for t in range(NT)])

            def last_expert():
                b, k, n = B - 1, E - 1, (E + 1) * B - 1
                dve.wait_ge(S["ya"], weighted(n - 1)[1])
                for h in range(2):
                    dve.wait_ge(S["ys"], n + 1 + h)
                    for t in range(HT * h, HT * (h + 1)):
                        V.scalar_tensor_tensor(out=acc[:, b, t], in0=ps[output_bank(n, t)][:, t * P:(t + 1) * P],
                                               scalar=CW[:, b, t, k:k + 1], in1=acc[:, b, t],
                                               op0=ALU.mult, op1=ALU.add).then_inc(S["ya"], 1)
                    dve.wait_ge(S["ya"], weighted(n, HT * (h + 1))[1])
                    stats(3, b, [acc[:, b, t] for t in range(NT)], HT * h, HT * (h + 1))

            def finish(b, t0=0, t1=NT):
                done = 2 * b + (2 if t0 else 0)
                dve.wait_ge(pw[3], b + (2 if t0 else 1))
                V.tensor_tensor(mh[:, b, t0:t1], MV[:, 3, b, t0:t1, 0], RS[:, 3, b, t0:t1],
                                ALU.mult).then_inc(S["mh_s"], 1)
                for t in range(t0, t1):
                    V.scalar_tensor_tensor(out=acc[:, b, t], in0=acc[:, b, t], scalar=RS[:, 3, b, t:t + 1],
                                           in1=TR[:, b, t], op0=ALU.mult, op1=ALU.add).then_inc(S["f1"], 1)
                    if t == t0:
                        dve.wait_ge(S["mh_s"], done + 1)
                        V.tensor_tensor(mh[:, b, t0:t1], NM[:, 1, b, t0:t1], mh[:, b, t0:t1],
                                        ALU.subtract).then_inc(S["mh_s"], 1)

            def silu_0(k):
                n, m = (0, 0) if k < 0 else (k + 2, k + 1)
                dve.wait_ge(S["th_s"], m + 1)
                if k >= 3:
                    dve.wait_ge(S["ys"], k - 1)
                V.scalar_tensor_tensor(out=hs0[:, k % 3 if k >= 0 else 3], in0=th[:, m % 2], scalar=1.0,
                                       in1=ps[hidden_bank(n)][:], op0=ALU.add, op1=ALU.mult).then_inc(S["sh0"], 1)

            def gated(b):
                n = (E + 2) * b + 1
                dve.wait_ge(S["h"], n + 1)
                wait_made(dve, b, -1)
                h_ = (hs0 if b == 0 else hs)[:, 3]
                V.scalar_tensor_tensor(out=h_, in0=h_, scalar=0.5 if b == 0 else 1.0, in1=ps[hidden_bank(n)][:],
                                       op0=ALU.mult, op1=ALU.mult).then_inc(S["hp"], 1)

            i = B - 1
            max_rows(i)
            silu_0(-1)
            x3_low(i - 2)
            gated(0)
            route2(i - 3)
            residual(i - 1)
            silu_0(0)
            residual2(i - 1)
            silu_0(1)
            route(i - 2)
            accumulate(0, 0)
            silu_0(2)
            neg_mean(2, i - 1)
            divide(i, 0)
            silu_0(3)
            accumulate(0, 2)
            divide(i, 1)
            route2(i - 2)
            accumulate(0, 4)
            x3_low(i - 1)
            route(i - 1)
            accumulate(0, 6)
            gated(1)
            accumulate(0, 7)
            add_other(0)
            norm_out(0)
            residual(B - 1)
            for b in range(1, B):
                accumulate(b, 0)
                if b == 1:
                    residual2(B - 1)
                accumulate(b, 2)
                if b == 1:
                    neg_mean(2, B - 1)
                    route2(B - 2)
                if b == B - 1:
                    finish(b - 1)
                accumulate(b, 4)
                if b < B - 1:
                    finish(b - 1)
                else:
                    add_other(b)
                    accumulate(b, 5)
                if b == 2:
                    route2(B - 1)
                accumulate(b, 6)
                if b == 1:
                    x3_low(B - 1)
                if b + 1 < B:
                    gated(b + 1)
                if b == B - 1:
                    last_expert()
                else:
                    accumulate(b, E - 1)
                    add_other(b)
                    norm_out(b)
                if b == 1:
                    route(B - 1)
            finish(B - 1, 0, HT)
            finish(B - 1, HT, NT)


def constants():
    import numpy as np
    c = np.zeros((P, C_END), np.float32)
    eye = np.eye(P, dtype=np.float32)
    c[:, C_ID:C_ID + P] = eye
    for g in range(G):
        for j in (0, 1, 4, 6):
            at = C_SEL + (g * 8 + j) * 32
            c[:, at:at + 32] = eye[:, 32 * g:32 * g + 32]
    p = np.arange(P)
    for h in range(HG):
        c[:MROW, C_HM + h] = (p[:MROW] % 32) // HD == h
    for h in range(H):
        c[MROW:, C_ONE + h] = (p[MROW:] - MROW) % H == h
    for j in range(2):
        half = (p // KEYS == j).astype(np.float32)
        c[:, C_VM + j] = half
        c[:, C_VB + 2 * HD + j] = half
    c[:, C_IO:C_IO + E] = np.arange(E)
    return c


_INS = ["L0_attn_x", "L0_attn_w_qkv", "L0_attn_w_out", "L0_ffn_router_w", "L0_ffn_w1", "L0_ffn_w2",
        "L0_ffn_shared_gate_up", "L0_ffn_shared_down", "L0_ffn_shared_gate_w"]


def kernel(**inputs):
    import numpy as np
    import concourse.bacc as bacc
    from concourse.bass_utils import run_bass_kernel_spmd as run

    nc = bacc.Bacc("TRN2", target_bir_lowering=False, num_devices=1)
    arrays, args = {}, []
    named = [(n, np.ascontiguousarray(inputs[n])) for n in _INS] + [("consts", constants())]
    for n, a in named:
        arrays[f"in_{n}"] = a
        args.append(nc.dram_tensor(f"in_{n}", a.shape, mybir.dt.from_np(a.dtype), kind="ExternalInput").ap())
    out = nc.dram_tensor("out", (B, T, D), F32, kind="ExternalOutput").ap()
    program(nc, *args, out)
    r = run(nc, [arrays], core_ids=[0])
    return r.results[0]["out"]
```
